# Optimizing a Trainium2 kernel written in Bass

```python
import numpy as np
import jax
import jax.numpy as jnp

def _softmax(x, axis=-1):
    return jax.nn.softmax(x, axis=axis)

def _gelu(x):
    return jax.nn.gelu(x, approximate=True)

def _silu(x):
    return jax.nn.silu(x)

def _sigmoid(x):
    return jax.nn.sigmoid(x)

def _layernorm(x, axis=-1, eps=1e-05):
    m = jnp.mean(x, axis=axis, keepdims=True)
    v = jnp.var(x, axis=axis, keepdims=True)
    return (x - m) / jnp.sqrt(v + eps)

def _scatter_add(tgt, idx, src, axis=0):
    return tgt.at[idx].add(src)

def _segment_sum(src, seg, n):
    return jax.ops.segment_sum(src, seg, n)
kernel_name = 'mk_dlrm_tower_d1_rec_r8_e9a13f'

def setup_inputs(seed: int=0):
    np.random.seed(seed)
    _w = jnp.asarray

    def _rec_inputs():
        import jax
        import jax.numpy as jnp
        _tk = jax.random.key(seed)
        ids = jnp.stack([jax.random.randint(jax.random.fold_in(_tk, 200 + f), (2048,), 0, v, jnp.int32) for f, v in enumerate([1000, 12500, 12500, 12500, 1000, 1000, 1000, 125000, 1000, 12500, 12500, 1250, 12500, 1000, 1000, 12500, 12500, 1000, 1250, 12500, 1000, 1000, 1250, 1000, 1250, 1000])], axis=1)
        tbl_0 = 0.05 * jax.random.normal(jax.random.fold_in(_tk, 500 + 0), (1000, 128), jnp.float32)
        tbl_1 = 0.05 * jax.random.normal(jax.random.fold_in(_tk, 500 + 1), (12500, 128), jnp.float32)
        tbl_2 = 0.05 * jax.random.normal(jax.random.fold_in(_tk, 500 + 2), (12500, 128), jnp.float32)
        tbl_3 = 0.05 * jax.random.normal(jax.random.fold_in(_tk, 500 + 3), (12500, 128), jnp.float32)
        tbl_4 = 0.05 * jax.random.normal(jax.random.fold_in(_tk, 500 + 4), (1000, 128), jnp.float32)
        tbl_5 = 0.05 * jax.random.normal(jax.random.fold_in(_tk, 500 + 5), (1000, 128), jnp.float32)
        tbl_6 = 0.05 * jax.random.normal(jax.random.fold_in(_tk, 500 + 6), (1000, 128), jnp.float32)
        tbl_7 = 0.05 * jax.random.normal(jax.random.fold_in(_tk, 500 + 7), (125000, 128), jnp.float32)
        tbl_8 = 0.05 * jax.random.normal(jax.random.fold_in(_tk, 500 + 8), (1000, 128), jnp.float32)
        tbl_9 = 0.05 * jax.random.normal(jax.random.fold_in(_tk, 500 + 9), (12500, 128), jnp.float32)
        tbl_10 = 0.05 * jax.random.normal(jax.random.fold_in(_tk, 500 + 10), (12500, 128), jnp.float32)
        tbl_11 = 0.05 * jax.random.normal(jax.random.fold_in(_tk, 500 + 11), (1250, 128), jnp.float32)
        tbl_12 = 0.05 * jax.random.normal(jax.random.fold_in(_tk, 500 + 12), (12500, 128), jnp.float32)
        tbl_13 = 0.05 * jax.random.normal(jax.random.fold_in(_tk, 500 + 13), (1000, 128), jnp.float32)
        tbl_14 = 0.05 * jax.random.normal(jax.random.fold_in(_tk, 500 + 14), (1000, 128), jnp.float32)
        tbl_15 = 0.05 * jax.random.normal(jax.random.fold_in(_tk, 500 + 15), (12500, 128), jnp.float32)
        tbl_16 = 0.05 * jax.random.normal(jax.random.fold_in(_tk, 500 + 16), (12500, 128), jnp.float32)
        tbl_17 = 0.05 * jax.random.normal(jax.random.fold_in(_tk, 500 + 17), (1000, 128), jnp.float32)
        tbl_18 = 0.05 * jax.random.normal(jax.random.fold_in(_tk, 500 + 18), (1250, 128), jnp.float32)
        tbl_19 = 0.05 * jax.random.normal(jax.random.fold_in(_tk, 500 + 19), (12500, 128), jnp.float32)
        tbl_20 = 0.05 * jax.random.normal(jax.random.fold_in(_tk, 500 + 20), (1000, 128), jnp.float32)
        tbl_21 = 0.05 * jax.random.normal(jax.random.fold_in(_tk, 500 + 21), (1000, 128), jnp.float32)
        tbl_22 = 0.05 * jax.random.normal(jax.random.fold_in(_tk, 500 + 22), (1250, 128), jnp.float32)
        tbl_23 = 0.05 * jax.random.normal(jax.random.fold_in(_tk, 500 + 23), (1000, 128), jnp.float32)
        tbl_24 = 0.05 * jax.random.normal(jax.random.fold_in(_tk, 500 + 24), (1250, 128), jnp.float32)
        tbl_25 = 0.05 * jax.random.normal(jax.random.fold_in(_tk, 500 + 25), (1000, 128), jnp.float32)
        _rk = jax.random.fold_in(_tk, 7)
        r_dense_features = 7.22013e-05 + 1.00017 * jax.random.normal(jax.random.fold_in(_rk, 101), (2048, 128), jnp.float32)
        W_top1 = 0.0456912 * jax.random.normal(jax.random.fold_in(_tk, 801), (479, 512), jnp.float32)
        W_top2 = 0.0441942 * jax.random.normal(jax.random.fold_in(_tk, 802), (512, 256), jnp.float32)
        W_top3 = 0.0625 * jax.random.normal(jax.random.fold_in(_tk, 803), (256, 1), jnp.float32)
        b_top1 = jnp.zeros((512,), jnp.float32)
        b_top2 = jnp.zeros((256,), jnp.float32)
        return (r_dense_features, ids, tbl_0, tbl_1, tbl_2, tbl_3, tbl_4, tbl_5, tbl_6, tbl_7, tbl_8, tbl_9, tbl_10, tbl_11, tbl_12, tbl_13, tbl_14, tbl_15, tbl_16, tbl_17, tbl_18, tbl_19, tbl_20, tbl_21, tbl_22, tbl_23, tbl_24, tbl_25, W_top1, b_top1, W_top2, b_top2, W_top3)
    r_dense_features, ids, tbl_0, tbl_1, tbl_2, tbl_3, tbl_4, tbl_5, tbl_6, tbl_7, tbl_8, tbl_9, tbl_10, tbl_11, tbl_12, tbl_13, tbl_14, tbl_15, tbl_16, tbl_17, tbl_18, tbl_19, tbl_20, tbl_21, tbl_22, tbl_23, tbl_24, tbl_25, W_top1, b_top1, W_top2, b_top2, W_top3 = _rec_inputs()

    def _L0_rec_setup():
        import jax, jax.numpy as jnp
        import numpy as np
        FEATURE_NUM = 27
        key = jax.random.key(seed)
        k1, k2 = jax.random.split(key)
        B, N, D = (8192, FEATURE_NUM - 1, 128)
        dense_features = jax.random.normal(k1, (B, D), dtype=jnp.float32)
        sparse_features = jax.random.normal(k2, (B, N, D), dtype=jnp.float32)
        return {'dense_features': dense_features, 'sparse_features': sparse_features}
    _L0_rec_all = _L0_rec_setup()
    _L0_rec_in = {k: v for k, v in _L0_rec_all.items() if k in ()}
    del _L0_rec_all
    return {'r_dense_features': r_dense_features, 'ids': ids, 'tbl_0': tbl_0, 'tbl_1': tbl_1, 'tbl_2': tbl_2, 'tbl_3': tbl_3, 'tbl_4': tbl_4, 'tbl_5': tbl_5, 'tbl_6': tbl_6, 'tbl_7': tbl_7, 'tbl_8': tbl_8, 'tbl_9': tbl_9, 'tbl_10': tbl_10, 'tbl_11': tbl_11, 'tbl_12': tbl_12, 'tbl_13': tbl_13, 'tbl_14': tbl_14, 'tbl_15': tbl_15, 'tbl_16': tbl_16, 'tbl_17': tbl_17, 'tbl_18': tbl_18, 'tbl_19': tbl_19, 'tbl_20': tbl_20, 'tbl_21': tbl_21, 'tbl_22': tbl_22, 'tbl_23': tbl_23, 'tbl_24': tbl_24, 'tbl_25': tbl_25, 'W_top1': W_top1, 'b_top1': b_top1, 'W_top2': W_top2, 'b_top2': b_top2, 'W_top3': W_top3}

def reference(r_dense_features, ids, tbl_0, tbl_1, tbl_2, tbl_3, tbl_4, tbl_5, tbl_6, tbl_7, tbl_8, tbl_9, tbl_10, tbl_11, tbl_12, tbl_13, tbl_14, tbl_15, tbl_16, tbl_17, tbl_18, tbl_19, tbl_20, tbl_21, tbl_22, tbl_23, tbl_24, tbl_25, W_top1, b_top1, W_top2, b_top2, W_top3):
    import jax
    import jax.numpy as jnp

    def _L0_rec_ref(dense_features, sparse_features):
        import jax, jax.numpy as jnp
        import numpy as np
        FEATURE_NUM = 27
        combined = jnp.concatenate([dense_features[:, None, :], sparse_features], axis=1)
        interactions = jnp.einsum('bfd,bgd->bfg', combined, combined)
        iu, ju = jnp.triu_indices(FEATURE_NUM, k=1)
        return interactions[:, iu, ju]
    e = jnp.stack([tbl_0[ids[:, 0]], tbl_1[ids[:, 1]], tbl_2[ids[:, 2]], tbl_3[ids[:, 3]], tbl_4[ids[:, 4]], tbl_5[ids[:, 5]], tbl_6[ids[:, 6]], tbl_7[ids[:, 7]], tbl_8[ids[:, 8]], tbl_9[ids[:, 9]], tbl_10[ids[:, 10]], tbl_11[ids[:, 11]], tbl_12[ids[:, 12]], tbl_13[ids[:, 13]], tbl_14[ids[:, 14]], tbl_15[ids[:, 15]], tbl_16[ids[:, 16]], tbl_17[ids[:, 17]], tbl_18[ids[:, 18]], tbl_19[ids[:, 19]], tbl_20[ids[:, 20]], tbl_21[ids[:, 21]], tbl_22[ids[:, 22]], tbl_23[ids[:, 23]], tbl_24[ids[:, 24]], tbl_25[ids[:, 25]]], axis=1)
    z = _L0_rec_ref(r_dense_features, e)
    z = z.reshape(z.shape[0], -1)
    h = jnp.concatenate([z, r_dense_features], axis=1)
    h = jnp.maximum(h @ W_top1 + b_top1, 0.0)
    h = jnp.maximum(h @ W_top2 + b_top2, 0.0)
    y = h @ W_top3
    return y

_drawn_inputs = setup_inputs


def setup_inputs(seed=0):
    import zlib

    import numpy as np

    out = dict(_drawn_inputs(seed))
    spreads = {'b_top1': (0.0, 0.1), 'b_top2': (0.0, 0.1)}
    factors = {}
    for name, (base, spread) in spreads.items():
        noise = np.random.default_rng([zlib.crc32(name.encode()), seed]).standard_normal(out[name].shape)
        drawn = base * np.exp(spread * noise) if base else spread * noise
        out[name] = jnp.asarray(drawn.astype(out[name].dtype))
    for name, factor in factors.items():
        out[name] = (out[name] * factor).astype(out[name].dtype)
    return out
```

```python
import concourse.bass as bass
from concourse import mybir
from contextlib import ExitStack


def dlrm_tower_kernel(nc, dense, ids, tables, w1, b1, w2, b2, w3, out):
    fp32 = mybir.dt.float32
    fp32r = mybir.dt.float32r
    i32 = mybir.dt.int32
    ALU = mybir.AluOpType
    ACT = mybir.ActivationFunctionType

    P = 128
    BATCH, D = dense.shape
    TABLES = len(tables)
    F = TABLES + 1
    HID1, HID2 = w2.shape
    QUADS = 4
    Q = P // QUADS
    HALVES = 4
    GROUP = HALVES * P
    GROUPS = BATCH // GROUP
    PAIRS = F * (F - 1) // 2
    ZC = 3
    ZK = PAIRS // ZC
    KC = ZC + 1
    M1, M2 = HID1 // P, HID2 // P
    BANK = 512
    PER = 4
    TB = -(-F // PER)
    TG = TB * HALVES
    NB = P // QUADS // 2
    ZB = -(-(F - 1) // PER)
    ZG = ZB + ZC
    MB = 1 + M1 + M2 + 1
    pair_at = [g * (g - 1) // 2 for g in range(F)]

    ctx = ExitStack()
    with ctx:
        def sb(name, shape, dt):
            return ctx.enter_context(nc.sbuf_tensor(name, shape, dt))

        def sem(name):
            return ctx.enter_context(nc.semaphore(name))

        identity = sb("identity", [P, P], fp32)
        ids_sb = sb("ids_sb", [P, HALVES, TABLES], i32)
        rows = sb("rows", [P, 2, F, D], fp32)
        features = sb("features", [P, 2, P * F + Q - F], fp32)
        gram = sb("gram", [P, F, P], fp32)
        pairs = sb("pairs", [P, QUADS, PAIRS], fp32)
        dense_rows = sb("dense_rows", [P, HALVES, D], fp32)
        x_hi = sb("x_hi", [P, KC, GROUP], fp32r)
        x_lo = sb("x_lo", [P, KC, GROUP], fp32r)
        w1_raw = sb("w1_raw", [P, KC, HID1], fp32)
        w1_hi = sb("w1_hi", [P, KC, HID1], fp32r)
        w1_lo = sb("w1_lo", [P, KC, HID1], fp32r)
        w2_raw = sb("w2_raw", [P, M1, HID2], fp32)
        w2_hi = sb("w2_hi", [P, M1, HID2], fp32r)
        w2_lo = sb("w2_lo", [P, M1, HID2], fp32r)
        w3_sb = sb("w3_sb", [P, M2], fp32)
        b1_sb = sb("b1_sb", [P, M1], fp32)
        b2_sb = sb("b2_sb", [P, M2], fp32)
        relu1 = sb("relu1", [P, 2, GROUP], fp32)
        h1_hi = sb("h1_hi", [P, M1, GROUP], fp32r)
        h1_lo = sb("h1_lo", [P, M1, GROUP], fp32r)
        h2 = sb("h2", [P, M2, GROUP], fp32)
        y_sb = sb("y_sb", [P, GROUPS * QUADS], fp32)

        feat_ps = ctx.enter_context(nc.psum_tensor("feat_ps", [P, 2, BANK], fp32))
        gram_ps = ctx.enter_context(nc.psum_tensor("gram_ps", [P, 2, BANK], fp32))
        pair_ps = ctx.enter_context(nc.psum_tensor("pair_ps", [P, 2, BANK], fp32))
        mlp_ps = ctx.enter_context(nc.psum_tensor("mlp_ps", [P, 2, BANK], fp32))

        ids_in = [sem(f"ids_in{h}") for h in range(HALVES)]
        dense_in = [sem(f"dense_in{s}") for s in range(2)]
        gathered = [[sem(f"gathered{s}_{k}") for k in range(TB)] for s in range(2)]
        gathers_begun = sem("gathers_begun")
        dense_rows_in = sem("dense_rows_in")
        weights_in = sem("weights_in")
        identity_zero = sem("identity_zero")
        identity_ready = sem("identity_ready")
        pad_ready = sem("pad_ready")
        weights_hi = sem("weights_hi")
        weights_split = sem("weights_split")
        feat_transposed = sem("feat_transposed")
        feat_copied = [sem(f"feat_copied{b}") for b in range(2)]
        gram_done = sem("gram_done")
        gram_copied = [sem(f"gram_copied{b}") for b in range(2)]
        pair_transposed = sem("pair_transposed")
        pair_copied = [sem(f"pair_copied{b}") for b in range(2)]
        x_hi_ready = sem("x_hi_ready")
        mlp_done = sem("mlp_done")
        mlp_copied = [sem(f"mlp_copied{b}") for b in range(2)]
        h1_hi_ready = sem("h1_hi_ready")
        h1_split = sem("h1_split")
        y_out = sem("y_out")

        block = ctx.enter_context(nc.Block())

        def wait(eng, semaphore, count):
            if not (isinstance(count, int) and count <= 0):
                eng.wait_ge(semaphore, count)

        def bank_features(k):
            return PER * k, min(F, PER * (k + 1))

        def features_by_feature(slot):
            return features[:, slot, 0:P * F].rearrange("p (b f) -> p f b", f=F)

        @block.sync
        def _(sp):
            def loads(G):
                for h in range(HALVES):
                    r0 = G * GROUP + h * P
                    wait(sp, feat_transposed, TG * G + TB * (h - 3))
                    sp.dma_start(ids_sb[:, h, :], ids[bass.ds(r0, P), :]).then_inc(ids_in[h], 16)
                    wait(sp, feat_transposed, TG * G + TB * (h - 2) + 1)
                    sp.dma_start(rows[:, h % 2, 0, :], dense[bass.ds(r0, P), :]).then_inc(dense_in[h % 2], 16)
                wait(sp, mlp_done, MB * (G - 1) + 1)
                sp.dma_start(dense_rows[:, :, :],
                             dense[bass.ds(G * GROUP, GROUP), :].rearrange("(h p) d -> p h d", p=P)
                             ).then_inc(dense_rows_in, 16)

            loads(0)
            with sp.Fori(1, GROUPS) as G:
                loads(G)

        @block.gpsimd
        def _(pool):
            nc.gpsimd.memset(identity[:, :], 0.0).then_inc(identity_zero, 1)
            pool.wait_ge(identity_zero, 1)
            nc.gpsimd.affine_select(out=identity[:, :], in_=identity[:, :], compare_op=ALU.not_equal, fill=1.0,
                                    base=0, pattern=[[-1, P]], channel_multiplier=1).then_inc(identity_ready, 1)

            def gathers(G):
                for h in range(HALVES):
                    pool.wait_ge(ids_in[h], 16 * G + 16)
                    for k in range(TB):
                        wait(pool, feat_transposed, TG * G + TB * (h - 2) + k + 1)
                        nc.gpsimd.sem_inc(gathers_begun, 1)
                        first, end = bank_features(k)
                        for f in range(max(first, 1), end):
                            nc.gpsimd.indirect_dma_start(
                                rows[:, h % 2, f, :], None, tables[f - 1],
                                bass.IndirectOffsetOnAxis(ids_sb[:, h, f - 1:f], 0)
                            ).then_inc(gathered[h % 2][k], 16)

            gathers(0)
            with pool.Fori(1, GROUPS) as G:
                gathers(G)

        @block.tensor
        def _(pe):
            def transpose_features(G, h):
                slot = h % 2
                use = 2 * G + h // 2 + 1
                for k in range(TB):
                    i = TB * h + k
                    first, end = bank_features(k)
                    if k == 0:
                        pe.wait_ge(dense_in[slot], 16 * use)
                    pe.wait_ge(gathered[slot][k], 16 * (end - max(first, 1)) * use)
                    wait(pe, feat_copied[i % 2], TG // 2 * G + i // 2)
                    for f in range(first, end):
                        last = nc.tensor.transpose(feat_ps[:, i % 2, (f - first) * P:(f - first + 1) * P],
                                                   rows[:, slot, f, :], identity[:, :])
                    last.then_inc(feat_transposed, 1)

            def gram_matrices(G, h):
                slot = h % 2
                done = TB * (h + 1)
                pe.wait_ge(feat_copied[0], TG // 2 * G + (done + 1) // 2)
                pe.wait_ge(feat_copied[1], TG // 2 * G + done // 2)
                for b in range(2):
                    wait(pe, gram_copied[b], HALVES * G + h)
                    for m in range(NB):
                        for s in range(QUADS):
                            at = (QUADS * (NB * b + m) + s) * F
                            last = nc.tensor.matmul(gram_ps[Q * s:Q * s + Q, b, m * F:(m + 1) * F],
                                                    features[:, slot, at:at + Q], features[:, slot, at:at + F],
                                                    start=True, stop=True)
                    last.then_inc(gram_done, 1)

            def pairs_to_rows(G):
                for b in range(2):
                    pe.wait_ge(gram_copied[b], HALVES * G + HALVES)
                for k in range(ZB):
                    if k >= 2:
                        pe.wait_ge(pair_copied[k % 2], ZG // 2 * G + k // 2)
                    for j, g in enumerate(range(1 + PER * k, min(F, 1 + PER * (k + 1)))):
                        last = nc.tensor.transpose(pair_ps[:, k % 2, j * P:(j + 1) * P], gram[:, g, :],
                                                   identity[:, :])
                    last.then_inc(pair_transposed, 1)

            def pairs_to_columns(G):
                pe.wait_ge(pair_copied[0], ZG // 2 * G + (ZB + 1) // 2)
                pe.wait_ge(pair_copied[1], ZG // 2 * G + ZB // 2)
                for c in range(ZC):
                    i = ZB + c
                    pe.wait_ge(pair_copied[i % 2], ZG // 2 * G + i // 2)
                    for s in range(QUADS):
                        last = nc.tensor.transpose(pair_ps[0:ZK, i % 2, s * P:(s + 1) * P],
                                                   pairs[:, s, c * ZK:(c + 1) * ZK], identity[:, :])
                    last.then_inc(pair_transposed, 1)
                pe.wait_ge(dense_rows_in, 16 * G + 16)
                for h in range(HALVES):
                    last = nc.tensor.transpose(mlp_ps[:, 0, h * P:(h + 1) * P], dense_rows[:, h, :], identity[:, :])
                last.then_inc(mlp_done, 1)

            def split_products(out, w_hi, w_lo, x_hi, x_lo, chunks, rows_of):
                steps = [(c, w, x) for c in range(chunks) for w, x in ((w_hi, x_hi), (w_hi, x_lo), (w_lo, x_hi))]
                for n, (c, w, x) in enumerate(steps):
                    k = rows_of(c)
                    last = nc.tensor.matmul(out, w(c, k), x[0:k, c, :], start=(n == 0), stop=(n == len(steps) - 1))
                return last

            def layer_1(G):
                for b in range(2):
                    pe.wait_ge(pair_copied[b], ZG // 2 * G + ZG // 2)
                pe.wait_ge(mlp_copied[0], MB // 2 * G + 1)
                for m in range(M1):
                    j = 1 + m
                    if m >= 1:
                        pe.wait_ge(mlp_copied[j % 2], MB // 2 * G + j // 2)
                    cols = slice(m * P, (m + 1) * P)
                    split_products(mlp_ps[:, j % 2, :], lambda c, k: w1_hi[0:k, c, cols],
                                   lambda c, k: w1_lo[0:k, c, cols], x_hi, x_lo, KC,
                                   lambda c: ZK if c < ZC else D).then_inc(mlp_done, 1)

            def layer_2(G):
                pe.wait_ge(h1_split, M1 * G + M1)
                for m in range(M2):
                    j = 1 + M1 + m
                    wait(pe, mlp_copied[j % 2], MB // 2 * G + j // 2)
                    cols = slice(m * P, (m + 1) * P)
                    split_products(mlp_ps[:, j % 2, :], lambda c, k: w2_hi[0:k, c, cols],
                                   lambda c, k: w2_lo[0:k, c, cols], h1_hi, h1_lo, M1,
                                   lambda c: P).then_inc(mlp_done, 1)

            def layer_3(G):
                j = MB - 1
                pe.wait_ge(mlp_copied[(j - 1) % 2], MB // 2 * G + (j - 1) // 2 + 1)
                pe.wait_ge(mlp_copied[j % 2], MB // 2 * G + j // 2)
                for s in range(QUADS):
                    for m in range(M2):
                        last = nc.tensor.matmul(mlp_ps[:, j % 2, s:s + 1], h2[:, m, s * P:(s + 1) * P],
                                                w3_sb[:, m:m + 1], start=(m == 0), stop=(m == M2 - 1))
                last.then_inc(mlp_done, 1)

            def group(G, before):
                for h, stage in enumerate((pairs_to_rows, pairs_to_columns, layer_1, layer_2)):
                    transpose_features(G, h)
                    if before is not None:
                        stage(before)
                    gram_matrices(G, h)
                if before is not None:
                    layer_3(before)

            pe.wait_ge(identity_ready, 1)
            pe.wait_ge(pad_ready, 1)
            group(0, None)
            pe.wait_ge(weights_split, 2)
            with pe.Fori(1, GROUPS) as G:
                group(G, G - 1)
            for stage in (pairs_to_rows, pairs_to_columns, layer_1, layer_2, layer_3):
                stage(GROUPS - 1)

        def copy_features(eng, copy, parity, G, h):
            for k in range(TB):
                i = TB * h + k
                if i % 2 != parity:
                    continue
                first, end = bank_features(k)
                eng.wait_ge(feat_transposed, TG * G + i + 1)
                wait(eng, gram_done, 2 * (HALVES * G + h - 1))
                copy(features_by_feature(h % 2)[:, first:end, :],
                     feat_ps[:, i % 2, 0:(end - first) * P].rearrange("p (f b) -> p f b", b=P)
                     ).then_inc(feat_copied[i % 2], 1)

        def copy_gram(eng, copy, b, G, h):
            eng.wait_ge(gram_done, 2 * HALVES * G + 2 * h + b + 1)
            wait(eng, pair_transposed, ZG * (G - 1) + ZB)
            n0 = h * Q + b * NB
            copy(gram[:, :, n0:n0 + NB], gram_ps[:, b, 0:NB * F].rearrange("p (n g) -> p g n", g=F)
                 ).then_inc(gram_copied[b], 1)

        def copy_pair_rows(eng, copy, parity, G):
            for k in range(parity, ZB, 2):
                eng.wait_ge(pair_transposed, ZG * G + k + 1)
                for j, g in enumerate(range(1 + PER * k, min(F, 1 + PER * (k + 1)))):
                    last = copy(pairs[:, :, pair_at[g]:pair_at[g] + g],
                                pair_ps[:, k % 2, j * P:(j + 1) * P].rearrange("p (s f) -> p s f", f=Q)[:, :, 0:g])
                last.then_inc(pair_copied[k % 2], 1)

        @block.scalar
        def _(act):
            def copy(dst, src):
                return nc.scalar.copy(dst, src)

            def split_x(G):
                for c in range(ZC):
                    act.wait_ge(pair_transposed, ZG * G + ZB + c + 1)
                    nc.scalar.copy(x_hi[0:ZK, c, :], pair_ps[0:ZK, (ZB + c) % 2, :]).then_inc(x_hi_ready, 1)
                act.wait_ge(mlp_done, MB * G + 1)
                nc.scalar.copy(x_hi[:, ZC, :].rearrange("p (s n) -> p s n", s=QUADS),
                               mlp_ps[:, 0, :].rearrange("p (n s) -> p s n", s=QUADS)).then_inc(x_hi_ready, 1)

            def relu_1(G):
                for m in range(M1):
                    j = 1 + m
                    act.wait_ge(mlp_done, MB * G + j + 1)
                    if m >= 2:
                        act.wait_ge(h1_split, M1 * G + m - 1)
                    nc.scalar.activation(relu1[:, m % 2, :], mlp_ps[:, j % 2, :], ACT.Relu,
                                         bias=b1_sb[:, m:m + 1]).then_inc(mlp_copied[j % 2], 1)
                    
            def relu_2(G):
                for m in range(M2):
                    j = 1 + M1 + m
                    act.wait_ge(mlp_done, MB * G + j + 1)
                    nc.scalar.activation(h2[:, m, :], mlp_ps[:, j % 2, :], ACT.Relu,
                                         bias=b2_sb[:, m:m + 1]).then_inc(mlp_copied[j % 2], 1)

            def store_y(G):
                act.wait_ge(mlp_done, MB * G + MB)
                nc.scalar.copy(y_sb[:, bass.ds(G * QUADS, QUADS)], mlp_ps[:, (MB - 1) % 2, 0:QUADS]
                               ).then_inc(mlp_copied[(MB - 1) % 2], 1)

            def pair_rows(G):
                copy_pair_rows(act, copy, 0, G)

            def group(G, before):
                for h, stage in enumerate((pair_rows, split_x, relu_1, relu_2)):
                    copy_features(act, copy, 0, G, h)
                    if before is not None:
                        stage(before)
                    copy_gram(act, copy, 0, G, h)
                if before is not None:
                    store_y(before)

            act.dma_start(w1_raw[0:ZK, 0:ZC, :], w1[0:PAIRS, :].rearrange("(c k) n -> k c n", k=ZK)).then_inc(weights_in, 16)
            act.dma_start(w1_raw[:, ZC, :], w1[PAIRS:PAIRS + D, :]).then_inc(weights_in, 16)
            act.dma_start(w2_raw[:, :, :], w2.rearrange("(c k) n -> k c n", k=P)).then_inc(weights_in, 16)
            act.dma_start(b1_sb[:, :], b1.rearrange("(m p) -> p m", p=P), allow_slow_non_contiguous=True).then_inc(weights_in, 16)
            act.dma_start(b2_sb[:, :], b2.rearrange("(m p) -> p m", p=P), allow_slow_non_contiguous=True).then_inc(weights_in, 16)
            act.dma_start(w3_sb[:, :], w3.rearrange("(m p) o -> p (m o)", p=P), allow_slow_non_contiguous=True).then_inc(weights_in, 16)
            act.wait_ge(weights_in, 6 * 16)
            nc.scalar.copy(w1_hi[0:ZK, 0:ZC, :], w1_raw[0:ZK, 0:ZC, :]).then_inc(weights_hi, 1)
            nc.scalar.copy(w1_hi[:, ZC, :], w1_raw[:, ZC, :]).then_inc(weights_hi, 1)
            nc.scalar.copy(w2_hi[:, :, :], w2_raw[:, :, :]).then_inc(weights_hi, 1)
            group(0, None)
            with act.Fori(1, GROUPS) as G:
                group(G, G - 1)
            for stage in (pair_rows, split_x, relu_1, relu_2, store_y):
                stage(GROUPS - 1)
            act.wait_ge(mlp_copied[(MB - 1) % 2], MB // 2 * GROUPS)
            act.dma_start(out.rearrange("(g n s) o -> n g (s o)", g=GROUPS, s=QUADS),
                          y_sb[:, :].rearrange("p (g s) -> p g s", g=GROUPS)).then_inc(y_out, 16)
            act.wait_ge(y_out, 16)

        @block.vector
        def _(dve):
            def copy(dst, src):
                return nc.vector.tensor_copy(dst, src)

            def low_part(lo, whole, hi):
                return nc.vector.tensor_tensor(lo, whole, hi.bitcast(fp32), ALU.subtract)

            def split_x(G):
                for c in range(ZC):
                    dve.wait_ge(x_hi_ready, KC * G + c + 1)
                    low_part(x_lo[0:ZK, c, :], pair_ps[0:ZK, (ZB + c) % 2, :], x_hi[0:ZK, c, :]
                             ).then_inc(pair_copied[(ZB + c) % 2], 1)
                dve.wait_ge(x_hi_ready, KC * G + KC)
                low_part(x_lo[:, ZC, :].rearrange("p (s n) -> p s n", s=QUADS),
                         mlp_ps[:, 0, :].rearrange("p (n s) -> p s n", s=QUADS),
                         x_hi[:, ZC, :].rearrange("p (s n) -> p s n", s=QUADS)).then_inc(mlp_copied[0], 1)

            def split_h1(G):
                for m in range(M1):
                    j = 1 + m
                    dve.wait_ge(mlp_copied[j % 2], MB // 2 * G + j // 2 + 1)
                    nc.vector.tensor_copy(h1_hi[:, m, :], relu1[:, m % 2, :]).then_inc(h1_hi_ready, 1)
                    dve.wait_ge(h1_hi_ready, M1 * G + m + 1)
                    low_part(h1_lo[:, m, :], relu1[:, m % 2, :], h1_hi[:, m, :]).then_inc(h1_split, 1)

            def pair_rows(G):
                copy_pair_rows(dve, copy, 1, G)

            def group(G, before):
                for h, stage in enumerate((pair_rows, split_x, split_h1, None)):
                    copy_features(dve, copy, 1, G, h)
                    if before is not None and stage is not None:
                        stage(before)
                    copy_gram(dve, copy, 1, G, h)

            for slot in range(2):
                last = nc.vector.memset(features[:, slot, P * F:], 0.0)
            last.then_inc(pad_ready, 1)
            dve.wait_ge(weights_hi, 3)
            low_part(w1_lo[0:ZK, 0:ZC, :], w1_raw[0:ZK, 0:ZC, :], w1_hi[0:ZK, 0:ZC, :])
            low_part(w1_lo[:, ZC, :], w1_raw[:, ZC, :], w1_hi[:, ZC, :]).then_inc(weights_split, 1)
            low_part(w2_lo[:, :, :], w2_raw[:, :, :], w2_hi[:, :, :]).then_inc(weights_split, 1)
            group(0, None)
            with dve.Fori(1, GROUPS) as G:
                group(G, G - 1)
            for stage in (pair_rows, split_x, split_h1):
                stage(GROUPS - 1)


def kernel(**inputs):
    import numpy as _np
    import concourse.bacc as _bacc
    from concourse import mybir as _mybir
    from concourse.bass_utils import run_bass_kernel_spmd as _run

    nc = _bacc.Bacc("TRN2", target_bir_lowering=False, num_devices=1)
    n_tables = sum(name.startswith("tbl_") for name in inputs)
    features = n_tables + 1
    row, col = _np.triu_indices(features, k=1)
    by_column = _np.lexsort((row, col))
    w1 = _np.ascontiguousarray(inputs["W_top1"])
    order = _np.concatenate([by_column, _np.arange(len(row), w1.shape[0])])
    arrays, aps = {}, {}

    def give(name, a):
        a = _np.ascontiguousarray(a)
        arrays[f"in_{name}"] = a
        aps[name] = nc.dram_tensor(f"in_{name}", a.shape, _mybir.dt.from_np(a.dtype), kind="ExternalInput").ap()
        return aps[name]

    dense = give("dense", inputs["r_dense_features"])
    ids = give("ids", inputs["ids"])
    tables = [give(f"tbl_{i}", inputs[f"tbl_{i}"]) for i in range(n_tables)]
    w1 = give("w1", w1[order])
    b1, w2, b2, w3 = (give(n, inputs[n]) for n in ("b_top1", "W_top2", "b_top2", "W_top3"))
    out = nc.dram_tensor("out_y", (inputs["ids"].shape[0], 1), _mybir.dt.float32, kind="ExternalOutput").ap()
    dlrm_tower_kernel(nc, dense, ids, tables, w1, b1, w2, b2, w3, out)
    r = _run(nc, [arrays], core_ids=[0])
    return r.results[0]["out_y"]
```

```python
import concourse.bass as bass
from concourse import mybir
from contextlib import ExitStack


def dlrm_tower_kernel(nc, dense, ids, gather_tables, ids_by_table, select_tables, w1, b1, w2, b2, w3, out):
    fp32 = mybir.dt.float32
    fp32r = mybir.dt.float32r
    i32 = mybir.dt.int32
    ALU = mybir.AluOpType
    ACT = mybir.ActivationFunctionType

    P = 128
    BATCH, D = dense.shape
    GATHERED = len(gather_tables)
    SELECTED = len(select_tables)
    RF = GATHERED + 1
    F = RF + SELECTED
    FC = F - 1
    HID1, HID2 = w2.shape
    QUADS = 4
    Q = P // QUADS
    HALVES = 4
    GROUP = HALVES * P
    GROUPS = BATCH // GROUP
    PAIRS = F * (F - 1) // 2
    ZC = 3
    ZK = PAIRS // ZC
    KC = ZC + 1
    M1, M2 = HID1 // P, HID2 // P
    BANK = 512
    PER = 4
    PAIR = 2 * P
    TB = -(-RF // PER)
    SB = -(-SELECTED // 2)
    PB = 2 * TB + SB
    TG = 2 * PB
    TR = select_tables[0].shape[0]
    CHUNKS = 8
    TP = TR // CHUNKS
    UNIT = 4
    RING = 4
    UNITS = SELECTED * CHUNKS // UNIT
    NB = P // QUADS // 2
    ZB = -(-FC // PER)
    ZG = ZB + ZC
    MB = 1 + M1 + M2 + 1
    pair_at = [g * (g - 1) // 2 for g in range(F)]

    ctx = ExitStack()
    with ctx:
        def sb(name, shape, dt):
            return ctx.enter_context(nc.sbuf_tensor(name, shape, dt))

        def sem(name):
            return ctx.enter_context(nc.semaphore(name))

        identity = sb("identity", [P, P], fp32)
        ids_sb = sb("ids_sb", [P, HALVES, GATHERED], i32)
        rows = sb("rows", [P, 2, RF, D], fp32)
        features = sb("features", [P, PAIR * F], fp32)
        gram = sb("gram", [P, FC, P], fp32)
        scratch = sb("scratch", [P, QUADS * PAIRS], fp32)
        pairs = scratch[:, :].rearrange("p (s z) -> p s z", s=QUADS)
        relu1 = scratch[:, 0:2 * GROUP].rearrange("p (a n) -> p a n", a=2)
        h2 = scratch[:, 0:M2 * GROUP].rearrange("p (m n) -> p m n", m=M2)
        STAGES = 3
        staging = [gram[:, 8 * i:8 * i + 8, :].rearrange("p a b -> p (a b)") for i in range(STAGES)]
        table_hi = sb("table_hi", [P, SELECTED, CHUNKS, D], fp32r)
        table_lo = sb("table_lo", [P, SELECTED, CHUNKS, D], fp32r)
        row_number_i = sb("row_number_i", [P, CHUNKS], i32)
        row_number = sb("row_number", [P, CHUNKS], fp32)
        ids_all = sb("ids_all", [P, SELECTED, PAIR], i32)
        one_hot = sb("one_hot", [P, RING, UNIT, PAIR], fp32r)
        dense_rows = sb("dense_rows", [P, HALVES, D], fp32)
        x_hi = sb("x_hi", [P, KC, GROUP], fp32r)
        x_lo = sb("x_lo", [P, KC, GROUP], fp32r)
        w1_hi = sb("w1_hi", [P, KC, HID1], fp32r)
        w1_lo = sb("w1_lo", [P, KC, HID1], fp32r)
        w2_hi = sb("w2_hi", [P, M1, HID2], fp32r)
        w2_lo = sb("w2_lo", [P, M1, HID2], fp32r)
        w3_sb = sb("w3_sb", [P, M2], fp32)
        b1_sb = sb("b1_sb", [P, M1], fp32)
        b2_sb = sb("b2_sb", [P, M2], fp32)
        h1_hi = sb("h1_hi", [P, M1, GROUP], fp32r)
        h1_lo = sb("h1_lo", [P, M1, GROUP], fp32r)
        y_sb = sb("y_sb", [P, GROUPS * QUADS], fp32)

        feat_ps = ctx.enter_context(nc.psum_tensor("feat_ps", [P, 2, BANK], fp32))
        gram_ps = ctx.enter_context(nc.psum_tensor("gram_ps", [P, 2, BANK], fp32))
        pair_ps = ctx.enter_context(nc.psum_tensor("pair_ps", [P, 2, BANK], fp32))
        mlp_ps = ctx.enter_context(nc.psum_tensor("mlp_ps", [P, 2, BANK], fp32))

        ids_in = [sem(f"ids_in{h}") for h in range(HALVES)]
        dense_in = [sem(f"dense_in{s}") for s in range(2)]
        gathered = [[sem(f"gathered{s}_{k}") for k in range(TB)] for s in range(2)]
        gathers_begun = sem("gathers_begun")
        loads_begun = sem("loads_begun")
        dense_rows_in = sem("dense_rows_in")
        biases_in = sem("biases_in")
        staged = [sem(f"staged{i}") for i in range(STAGES)]
        ids_all_in = sem("ids_all_in")
        row_number_written = sem("row_number_written")
        row_number_ready = sem("row_number_ready")
        one_hot_ready = sem("one_hot_ready")
        one_hot_used = sem("one_hot_used")
        identity_zero = sem("identity_zero")
        identity_ready = sem("identity_ready")
        gram_cleared = sem("gram_cleared")
        staged_hi = sem("staged_hi")
        staged_split = sem("staged_split")
        rows_transposed = sem("rows_transposed")
        feat_copied = [sem(f"feat_copied{b}") for b in range(2)]
        gram_done = sem("gram_done")
        gram_copied = [sem(f"gram_copied{b}") for b in range(2)]
        pair_transposed = sem("pair_transposed")
        pair_copied = [sem(f"pair_copied{b}") for b in range(2)]
        x_hi_ready = sem("x_hi_ready")
        mlp_done = sem("mlp_done")
        mlp_copied = [sem(f"mlp_copied{b}") for b in range(2)]
        h1_hi_ready = sem("h1_hi_ready")
        h1_split = sem("h1_split")
        y_out = sem("y_out")

        block = ctx.enter_context(nc.Block())

        def wait(eng, semaphore, count):
            if not (isinstance(count, int) and count <= 0):
                eng.wait_ge(semaphore, count)

        def bank_features(k):
            return PER * k, min(RF, PER * (k + 1))

        def row_bank(h, k):
            return PB * (h // 2) + (h % 2) * (TB + SB) + k

        def selected_bank(h, k):
            return PB * (h // 2) + TB + k

        features_by_feature = features[:, :].rearrange("p (b f) -> p f b", f=F)

        def as_chunks(c, n, parts=P):
            return lambda slot: slot[0:parts, 0:c * n].rearrange("p (c n) -> p c n", c=c)

        to_split = [([(select_tables[x].rearrange("(p c) d -> p c d", c=CHUNKS), as_chunks(CHUNKS, D, TP))],
                     as_chunks(CHUNKS, D, TP), table_hi[0:TP, x], table_lo[0:TP, x]) for x in range(SELECTED)]
        w1_pairs = w1[0:PAIRS, :].rearrange("(c k) n -> k c n", k=ZK)
        to_split += [([(w1_pairs[:, 0:2, :], as_chunks(2, HID1, ZK))],
                      as_chunks(2, HID1, ZK), w1_hi[0:ZK, 0:2, :], w1_lo[0:ZK, 0:2, :]),
                     ([(w1_pairs[:, 2, :], lambda slot: slot[0:ZK, 0:HID1])],
                      lambda slot: slot[0:ZK, 0:HID1], w1_hi[0:ZK, 2, :], w1_lo[0:ZK, 2, :]),
                     ([(w1[PAIRS:PAIRS + D, :], lambda slot: slot[:, 0:HID1])],
                      lambda slot: slot[:, 0:HID1], w1_hi[:, ZC, :], w1_lo[:, ZC, :]),
                     ([(w2.rearrange("(c k) n -> k c n", k=P), as_chunks(M1, HID2))],
                      as_chunks(M1, HID2), w2_hi[:, :, :], w2_lo[:, :, :])]

        @block.sync
        def _(sp):
            def wait_apart(semaphore, count):
                wait(sp, semaphore, count)
                sp.sem_inc(loads_begun, 1)

            def load_half(G, h):
                r0 = G * GROUP + h * P
                wait_apart(rows_transposed, TB * (HALVES * G + h - 3))
                sp.dma_start(ids_sb[:, h, :], ids[bass.ds(r0, P), :]).then_inc(ids_in[h], 16)
                wait_apart(rows_transposed, TB * (HALVES * G + h - 2) + 1)
                sp.dma_start(rows[:, h % 2, 0, :], dense[bass.ds(r0, P), :]).then_inc(dense_in[h % 2], 16)

            def load_ids_all(G, j):
                r0 = G * GROUP + j * PAIR
                wait_apart(one_hot_ready, UNITS * (2 * G + j))
                sp.dma_start(ids_all[:, :, :],
                             ids_by_table[:, bass.ds(r0, PAIR)].partition_broadcast(P)
                             ).then_inc(ids_all_in, 16)

            def load_dense_rows(G):
                r0 = G * GROUP
                wait_apart(mlp_done, MB * (G - 1) + 1)
                sp.dma_start(dense_rows[:, :, :],
                             dense[bass.ds(r0, GROUP), :].rearrange("(h p) d -> p h d", p=P)
                             ).then_inc(dense_rows_in, 16)

            load_half(0, 0)
            load_half(0, 1)
            load_ids_all(0, 0)
            for n, (sources, _, _, _) in enumerate(to_split):
                wait(sp, staged_split, n - STAGES + 1)
                for src, view in sources:
                    sp.dma_start(view(staging[n % STAGES]), src).then_inc(staged[n % STAGES], 16)
            load_half(0, 2)
            load_half(0, 3)
            load_ids_all(0, 1)
            load_dense_rows(0)
            with sp.Fori(1, GROUPS) as G:
                load_half(G, 0)
                load_ids_all(G, 0)
                load_half(G, 1)
                load_half(G, 2)
                load_ids_all(G, 1)
                load_half(G, 3)
                load_dense_rows(G)

        @block.gpsimd
        def _(pool):
            nc.gpsimd.memset(identity[:, :], 0.0).then_inc(identity_zero, 1)
            pool.wait_ge(identity_zero, 1)
            nc.gpsimd.affine_select(out=identity[:, :], in_=identity[:, :], compare_op=ALU.not_equal, fill=1.0,
                                    base=0, pattern=[[-1, P]], channel_multiplier=1).then_inc(identity_ready, 1)

            nc.gpsimd.iota(row_number_i[:, :], pattern=[[1, CHUNKS]], base=0, channel_multiplier=CHUNKS
                           ).then_inc(row_number_written, 1)

            def gathers(G):
                for h in range(HALVES):
                    pool.wait_ge(ids_in[h], 16 * G + 16)
                    for k in range(TB):
                        wait(pool, rows_transposed, TB * (HALVES * G + h - 2) + k + 1)
                        nc.gpsimd.sem_inc(gathers_begun, 1)
                        first, end = bank_features(k)
                        for f in range(max(first, 1), end):
                            nc.gpsimd.indirect_dma_start(
                                rows[:, h % 2, f, :], None, gather_tables[f - 1],
                                bass.IndirectOffsetOnAxis(ids_sb[:, h, f - 1:f], 0)
                            ).then_inc(gathered[h % 2][k], 16)

            gathers(0)
            with pool.Fori(1, GROUPS) as G:
                gathers(G)

        @block.tensor
        def _(pe):
            def transpose_features(G, h):
                slot = h % 2
                use = 2 * G + h // 2 + 1
                for k in range(TB):
                    i = row_bank(h, k)
                    first, end = bank_features(k)
                    if k == 0:
                        pe.wait_ge(dense_in[slot], 16 * use)
                    pe.wait_ge(gathered[slot][k], 16 * (end - max(first, 1)) * use)
                    wait(pe, feat_copied[i % 2], TG // 2 * G + i // 2)
                    for f in range(first, end):
                        last = nc.tensor.transpose(feat_ps[:, i % 2, (f - first) * P:(f - first + 1) * P],
                                                   rows[:, slot, f, :], identity[:, :])
                    last.then_inc(rows_transposed, 1)

            def select_rows(G, h):
                for x in range(SELECTED):
                    i = selected_bank(h, x // 2)
                    if x % 2 == 0:
                        wait(pe, feat_copied[i % 2], TG // 2 * G + i // 2)
                    out = feat_ps[:, i % 2, (x % 2) * PAIR:(x % 2 + 1) * PAIR]
                    for c in range(CHUNKS):
                        u = UNITS * (h // 2) + (x * CHUNKS + c) // UNIT
                        if c % UNIT == 0:
                            pe.wait_ge(one_hot_ready, 2 * UNITS * G + u + 1)
                        for table in (table_hi, table_lo):
                            last = nc.tensor.matmul(out, table[0:TP, x, c, :], one_hot[0:TP, u % RING, c % UNIT, :],
                                                    start=(c == 0 and table is table_hi),
                                                    stop=(c == CHUNKS - 1 and table is table_lo))
                        if c % UNIT == UNIT - 1:
                            last.then_inc(one_hot_used, 1)

            def gram_matrices(G, h):
                done = PB * (h // 2) + TB + SB if h % 2 == 0 else PB * (h // 2 + 1)
                pe.wait_ge(feat_copied[0], TG // 2 * G + (done + 1) // 2)
                pe.wait_ge(feat_copied[1], TG // 2 * G + done // 2)
                for b in range(2):
                    wait(pe, gram_copied[b], HALVES * G + h)
                    for m in range(NB):
                        for s in range(QUADS):
                            at = (P * (h % 2) + QUADS * (NB * b + m) + s) * F
                            last = nc.tensor.matmul(gram_ps[Q * s:Q * s + FC, b, m * FC:(m + 1) * FC],
                                                    features[:, at:at + FC], features[:, at + 1:at + F],
                                                    start=True, stop=True)
                    last.then_inc(gram_done, 1)

            def pairs_to_rows(G):
                for b in range(2):
                    pe.wait_ge(gram_copied[b], HALVES * G + HALVES)
                for k in range(ZB):
                    if k >= 2:
                        pe.wait_ge(pair_copied[k % 2], ZG // 2 * G + k // 2)
                    for j, g in enumerate(range(1 + PER * k, min(F, 1 + PER * (k + 1)))):
                        last = nc.tensor.transpose(pair_ps[:, k % 2, j * P:(j + 1) * P], gram[:, g - 1, :],
                                                   identity[:, :])
                    last.then_inc(pair_transposed, 1)

            def pairs_to_columns(G):
                pe.wait_ge(pair_copied[0], ZG // 2 * G + (ZB + 1) // 2)
                pe.wait_ge(pair_copied[1], ZG // 2 * G + ZB // 2)
                for c in range(ZC):
                    i = ZB + c
                    pe.wait_ge(pair_copied[i % 2], ZG // 2 * G + i // 2)
                    for s in range(QUADS):
                        last = nc.tensor.transpose(pair_ps[0:ZK, i % 2, s * P:(s + 1) * P],
                                                   pairs[:, s, c * ZK:(c + 1) * ZK], identity[:, :])
                    last.then_inc(pair_transposed, 1)
                pe.wait_ge(dense_rows_in, 16 * G + 16)
                for h in range(HALVES):
                    last = nc.tensor.transpose(mlp_ps[:, 0, h * P:(h + 1) * P], dense_rows[:, h, :], identity[:, :])
                last.then_inc(mlp_done, 1)

            def split_products(out, w_hi, w_lo, x_hi, x_lo, chunks, rows_of):
                steps = [(c, w, x) for c in range(chunks) for w, x in ((w_hi, x_hi), (w_hi, x_lo), (w_lo, x_hi))]
                for n, (c, w, x) in enumerate(steps):
                    k = rows_of(c)
                    last = nc.tensor.matmul(out, w(c, k), x[0:k, c, :], start=(n == 0), stop=(n == len(steps) - 1))
                return last

            def layer_1(G):
                for b in range(2):
                    pe.wait_ge(pair_copied[b], ZG // 2 * G + ZG // 2)
                pe.wait_ge(mlp_copied[0], MB // 2 * G + 1)
                for m in range(M1):
                    j = 1 + m
                    if m >= 1:
                        pe.wait_ge(mlp_copied[j % 2], MB // 2 * G + j // 2)
                    cols = slice(m * P, (m + 1) * P)
                    split_products(mlp_ps[:, j % 2, :], lambda c, k: w1_hi[0:k, c, cols],
                                   lambda c, k: w1_lo[0:k, c, cols], x_hi, x_lo, KC,
                                   lambda c: ZK if c < ZC else D).then_inc(mlp_done, 1)

            def layer_2(G):
                pe.wait_ge(h1_split, M1 * G + M1)
                for m in range(M2):
                    j = 1 + M1 + m
                    wait(pe, mlp_copied[j % 2], MB // 2 * G + j // 2)
                    cols = slice(m * P, (m + 1) * P)
                    split_products(mlp_ps[:, j % 2, :], lambda c, k: w2_hi[0:k, c, cols],
                                   lambda c, k: w2_lo[0:k, c, cols], h1_hi, h1_lo, M1,
                                   lambda c: P).then_inc(mlp_done, 1)

            def layer_3(G):
                j = MB - 1
                pe.wait_ge(mlp_copied[(j - 1) % 2], MB // 2 * G + (j - 1) // 2 + 1)
                pe.wait_ge(mlp_copied[j % 2], MB // 2 * G + j // 2)
                for s in range(QUADS):
                    for m in range(M2):
                        last = nc.tensor.matmul(mlp_ps[:, j % 2, s:s + 1], h2[:, m, s * P:(s + 1) * P],
                                                w3_sb[:, m:m + 1], start=(m == 0), stop=(m == M2 - 1))
                last.then_inc(mlp_done, 1)

            def group(G, before):
                for h, stage in enumerate((pairs_to_rows, pairs_to_columns, layer_1, layer_2)):
                    transpose_features(G, h)
                    if before is not None:
                        stage(before)
                    if h % 2 == 0:
                        select_rows(G, h)
                    gram_matrices(G, h)
                if before is not None:
                    layer_3(before)

            pe.wait_ge(identity_ready, 1)
            pe.wait_ge(gram_cleared, 1)
            pe.wait_ge(staged_split, len(to_split))
            pe.wait_ge(biases_in, 3 * 16)
            group(0, None)
            with pe.Fori(1, GROUPS) as G:
                group(G, G - 1)
            for stage in (pairs_to_rows, pairs_to_columns, layer_1, layer_2, layer_3):
                stage(GROUPS - 1)

        def copy_features(eng, copy, parity, G, h):
            for k in range(TB):
                i = row_bank(h, k)
                if i % 2 != parity:
                    continue
                first, end = bank_features(k)
                eng.wait_ge(rows_transposed, TB * (HALVES * G + h) + k + 1)
                wait(eng, gram_done, 2 * (HALVES * G + h - 1))
                copy(features_by_feature[:, first:end, (h % 2) * P:(h % 2 + 1) * P],
                     feat_ps[:, i % 2, 0:(end - first) * P].rearrange("p (f b) -> p f b", b=P)
                     ).then_inc(feat_copied[i % 2], 1)

        def copy_gram(eng, copy, b, G, h):
            eng.wait_ge(gram_done, 2 * HALVES * G + 2 * h + b + 1)
            wait(eng, pair_transposed, ZG * (G - 1) + ZB)
            n0 = h * Q + b * NB
            copy(gram[:, :, n0:n0 + NB], gram_ps[:, b, 0:NB * FC].rearrange("p (n g) -> p g n", g=FC)
                 ).then_inc(gram_copied[b], 1)

        def copy_pair_rows(eng, copy, parity, G):
            for k in range(parity, ZB, 2):
                eng.wait_ge(pair_transposed, ZG * G + k + 1)
                for j, g in enumerate(range(1 + PER * k, min(F, 1 + PER * (k + 1)))):
                    last = copy(pairs[:, :, pair_at[g]:pair_at[g] + g],
                                pair_ps[:, k % 2, j * P:(j + 1) * P].rearrange("p (s f) -> p s f", f=Q)[:, :, 0:g])
                last.then_inc(pair_copied[k % 2], 1)

        @block.scalar
        def _(act):
            def copy(dst, src):
                return nc.scalar.copy(dst, src)

            def split_x(G):
                for c in range(ZC):
                    act.wait_ge(pair_transposed, ZG * G + ZB + c + 1)
                    nc.scalar.copy(x_hi[0:ZK, c, :], pair_ps[0:ZK, (ZB + c) % 2, :]).then_inc(x_hi_ready, 1)
                act.wait_ge(mlp_done, MB * G + 1)
                nc.scalar.copy(x_hi[:, ZC, :].rearrange("p (s n) -> p s n", s=QUADS),
                               mlp_ps[:, 0, :].rearrange("p (n s) -> p s n", s=QUADS)).then_inc(x_hi_ready, 1)

            def relu_1(G):
                for m in range(M1):
                    j = 1 + m
                    act.wait_ge(mlp_done, MB * G + j + 1)
                    if m >= 2:
                        act.wait_ge(h1_split, M1 * G + m - 1)
                    nc.scalar.activation(relu1[:, m % 2, :], mlp_ps[:, j % 2, :], ACT.Relu,
                                         bias=b1_sb[:, m:m + 1]).then_inc(mlp_copied[j % 2], 1)
                    
            def relu_2(G):
                for m in range(M2):
                    j = 1 + M1 + m
                    act.wait_ge(mlp_done, MB * G + j + 1)
                    nc.scalar.activation(h2[:, m, :], mlp_ps[:, j % 2, :], ACT.Relu,
                                         bias=b2_sb[:, m:m + 1]).then_inc(mlp_copied[j % 2], 1)

            def store_y(G):
                act.wait_ge(mlp_done, MB * G + MB)
                nc.scalar.copy(y_sb[:, bass.ds(G * QUADS, QUADS)], mlp_ps[:, (MB - 1) % 2, 0:QUADS]
                               ).then_inc(mlp_copied[(MB - 1) % 2], 1)

            def copy_selected(G, h):
                for k in range(SB):
                    i = selected_bank(h, k)
                    n = min(2, SELECTED - 2 * k)
                    act.wait_ge(one_hot_used, 2 * UNITS * G + UNITS * (h // 2) + (2 * k + n) * CHUNKS // UNIT)
                    wait(act, gram_done, 2 * (HALVES * G + h))
                    nc.scalar.copy(features_by_feature[:, RF + 2 * k:RF + 2 * k + n, :],
                                   feat_ps[:, i % 2, 0:n * PAIR].rearrange("p (f b) -> p f b", b=PAIR)
                                   ).then_inc(feat_copied[i % 2], 1)

            def pair_rows(G):
                copy_pair_rows(act, copy, 0, G)

            def group(G, before):
                for h, stage in enumerate((pair_rows, split_x, relu_1, relu_2)):
                    copy_features(act, copy, 0, G, h)
                    if before is not None:
                        stage(before)
                    if h % 2 == 0:
                        copy_selected(G, h)
                    copy_gram(act, copy, 0, G, h)
                if before is not None:
                    store_y(before)

            act.dma_start(b1_sb[:, :], b1.rearrange("(m p) -> p m", p=P), allow_slow_non_contiguous=True).then_inc(biases_in, 16)
            act.dma_start(b2_sb[:, :], b2.rearrange("(m p) -> p m", p=P), allow_slow_non_contiguous=True).then_inc(biases_in, 16)
            act.dma_start(w3_sb[:, :], w3.rearrange("(m p) o -> p (m o)", p=P), allow_slow_non_contiguous=True).then_inc(biases_in, 16)
            for n, (_, view, hi, _) in enumerate(to_split):
                act.wait_ge(staged[n % STAGES], 16 * (n // STAGES + 1))
                nc.scalar.copy(hi, view(staging[n % STAGES])).then_inc(staged_hi, 1)
            act.wait_ge(biases_in, 3 * 16)
            group(0, None)
            with act.Fori(1, GROUPS) as G:
                group(G, G - 1)
            for stage in (pair_rows, split_x, relu_1, relu_2, store_y):
                stage(GROUPS - 1)
            act.wait_ge(mlp_copied[(MB - 1) % 2], MB // 2 * GROUPS)
            act.dma_start(out.rearrange("(g n s) o -> n g (s o)", g=GROUPS, s=QUADS),
                          y_sb[:, :].rearrange("p (g s) -> p g s", g=GROUPS)).then_inc(y_out, 16)
            act.wait_ge(y_out, 16)

        @block.vector
        def _(dve):
            def copy(dst, src):
                return nc.vector.tensor_copy(dst, src)

            def low_part(lo, whole, hi):
                return nc.vector.tensor_tensor(lo, whole, hi.bitcast(fp32), ALU.subtract)

            def split_x(G):
                for c in range(ZC):
                    dve.wait_ge(x_hi_ready, KC * G + c + 1)
                    low_part(x_lo[0:ZK, c, :], pair_ps[0:ZK, (ZB + c) % 2, :], x_hi[0:ZK, c, :]
                             ).then_inc(pair_copied[(ZB + c) % 2], 1)
                dve.wait_ge(x_hi_ready, KC * G + KC)
                low_part(x_lo[:, ZC, :].rearrange("p (s n) -> p s n", s=QUADS),
                         mlp_ps[:, 0, :].rearrange("p (n s) -> p s n", s=QUADS),
                         x_hi[:, ZC, :].rearrange("p (s n) -> p s n", s=QUADS)).then_inc(mlp_copied[0], 1)

            def split_h1(G):
                for m in range(M1):
                    j = 1 + m
                    dve.wait_ge(mlp_copied[j % 2], MB // 2 * G + j // 2 + 1)
                    nc.vector.tensor_copy(h1_hi[:, m, :], relu1[:, m % 2, :]).then_inc(h1_hi_ready, 1)
                    dve.wait_ge(h1_hi_ready, M1 * G + m + 1)
                    low_part(h1_lo[:, m, :], relu1[:, m % 2, :], h1_hi[:, m, :]).then_inc(h1_split, 1)

            def pair_rows(G):
                copy_pair_rows(dve, copy, 1, G)

            def write_one_hot(G, h, units):
                for v in units:
                    u = UNITS * (h // 2) + v
                    if v == 0:
                        dve.wait_ge(ids_all_in, 16 * (2 * G + h // 2 + 1))
                    wait(dve, one_hot_used, 2 * UNITS * G + u - RING + 1)
                    for c in range(UNIT):
                        x, chunk = (v * UNIT + c) // CHUNKS, (v * UNIT + c) % CHUNKS
                        last = nc.vector.tensor_scalar(one_hot[0:TP, u % RING, c, :], ids_all[0:TP, x, :],
                                                       row_number[0:TP, chunk:chunk + 1], None, ALU.is_equal)
                    last.then_inc(one_hot_ready, 1)

            def group(G, before):
                for h, stage in enumerate((pair_rows, split_x, split_h1, None)):
                    copy_features(dve, copy, 1, G, h)
                    if h % 2 == 0:
                        write_one_hot(G, h, range(RING))
                    if before is not None and stage is not None:
                        stage(before)
                    if h % 2 == 0:
                        write_one_hot(G, h, range(RING, UNITS))
                    copy_gram(dve, copy, 1, G, h)

            nc.vector.memset(gram_ps[:, :, :], 0.0).then_inc(gram_cleared, 1)
            for n, (_, view, hi, lo) in enumerate(to_split):
                dve.wait_ge(staged_hi, n + 1)
                low_part(lo, view(staging[n % STAGES]), hi).then_inc(staged_split, 1)
            dve.wait_ge(row_number_written, 1)
            nc.vector.tensor_copy(row_number[:, :], row_number_i[:, :]).then_inc(row_number_ready, 1)
            dve.wait_ge(row_number_ready, 1)
            group(0, None)
            with dve.Fori(1, GROUPS) as G:
                group(G, G - 1)
            for stage in (pair_rows, split_x, split_h1):
                stage(GROUPS - 1)


SELECT_TABLES, SELECT_ROWS = 7, 1000


def kernel(**inputs):
    import numpy as _np
    import concourse.bacc as _bacc
    from concourse import mybir as _mybir
    from concourse.bass_utils import run_bass_kernel_spmd as _run

    nc = _bacc.Bacc("TRN2", target_bir_lowering=False, num_devices=1)
    n_tables = sum(name.startswith("tbl_") for name in inputs)
    small = [t for t in range(n_tables) if inputs[f"tbl_{t}"].shape[0] == SELECT_ROWS]
    selected = small[:SELECT_TABLES]
    gathered = [t for t in range(n_tables) if t not in selected]
    feature = [0] + [t + 1 for t in gathered + selected]
    n = len(feature)
    order = []
    for g in range(n):
        for f in range(g):
            a, b = sorted((feature[f], feature[g]))
            order.append(a * n - a * (a + 1) // 2 + b - a - 1)
    w1 = _np.ascontiguousarray(inputs["W_top1"])
    order = _np.array(order + list(range(len(order), w1.shape[0])))
    arrays = {}

    def give(name, a):
        a = _np.ascontiguousarray(a)
        arrays[f"in_{name}"] = a
        return nc.dram_tensor(f"in_{name}", a.shape, _mybir.dt.from_np(a.dtype), kind="ExternalInput").ap()

    all_ids = _np.ascontiguousarray(inputs["ids"])
    dense = give("dense", inputs["r_dense_features"])
    ids = give("ids", all_ids[:, gathered])
    ids_by_table = give("ids_by_table", all_ids[:, selected].T)
    gather_tables = [give(f"tbl_{t}", inputs[f"tbl_{t}"]) for t in gathered]
    select_tables = [give(f"tbl_{t}", inputs[f"tbl_{t}"]) for t in selected]
    w1 = give("w1", w1[order])
    b1, w2, b2, w3 = (give(n, inputs[n]) for n in ("b_top1", "W_top2", "b_top2", "W_top3"))
    out = nc.dram_tensor("out_y", (all_ids.shape[0], 1), _mybir.dt.float32, kind="ExternalOutput").ap()
    dlrm_tower_kernel(nc, dense, ids, gather_tables, ids_by_table, select_tables, w1, b1, w2, b2, w3, out)
    r = _run(nc, [arrays], core_ids=[0])
    return r.results[0]["out_y"]
```

```python
import concourse.bass as bass
from concourse import mybir
from contextlib import ExitStack


def dlrm_tower_kernel(nc, dense, ids, gather_tables, ids_by_table, select_tables, w1, b1, w2, b2, w3, out):
    fp32 = mybir.dt.float32
    fp32r = mybir.dt.float32r
    i32 = mybir.dt.int32
    ALU = mybir.AluOpType
    ACT = mybir.ActivationFunctionType

    P = 128
    BATCH, D = dense.shape
    GATHERED = len(gather_tables)
    SELECTED = len(select_tables)
    RF = GATHERED + 1
    F = RF + SELECTED
    FC = F - 1
    HID1, HID2 = w2.shape
    QUADS = 4
    Q = P // QUADS
    HALVES = 4
    GROUP = HALVES * P
    GROUPS = BATCH // GROUP
    BATCHES = GROUPS + 1
    PAIRS = F * (F - 1) // 2
    ZC = 3
    ZK = PAIRS // ZC
    KC = ZC + 1
    M1, M2 = HID1 // P, HID2 // P
    BANK = 512
    PER = 4
    PAIR = 2 * P
    TB = -(-RF // PER)
    SB = -(-SELECTED // 2)
    PB = SB + 2 * TB
    TG = 2 * PB
    FB = 4
    TR = select_tables[0].shape[0]
    CHUNKS = 8
    TP = TR // CHUNKS
    UNIT = 2
    RING = 4
    UNITS = SELECTED * CHUNKS // UNIT
    NB = P // QUADS // 2
    ZB = -(-FC // PER)
    DENSE = ZB
    TO_COLUMNS = DENSE + 1
    LAYER_1 = TO_COLUMNS + ZC
    LAYER_2 = LAYER_1 + M1
    LAYER_3 = LAYER_2 + M2
    SG = LAYER_3 + 1
    assert SB == 4 and TG % FB == 0 and SG % 2 == 0 and 2 * UNITS % RING == 0
    pair_at = [g * (g - 1) // 2 for g in range(F)]

    ctx = ExitStack()
    with ctx:
        def sb(name, shape, dt):
            return ctx.enter_context(nc.sbuf_tensor(name, shape, dt))

        def sem(name):
            return ctx.enter_context(nc.semaphore(name))

        identity = sb("identity", [P, P], fp32)
        ids_sb = sb("ids_sb", [P, HALVES, GATHERED], i32)
        rows = sb("rows", [P, 2, RF, D], fp32)
        features = sb("features", [P, PAIR * F], fp32)
        gram = sb("gram", [P, FC, P], fp32)
        scratch = sb("scratch", [P, QUADS * PAIRS], fp32)
        pairs = scratch[:, :].rearrange("p (s z) -> p s z", s=QUADS)
        relu1 = scratch[:, 0:2 * GROUP].rearrange("p (a n) -> p a n", a=2)
        h2 = scratch[:, 0:M2 * GROUP].rearrange("p (m n) -> p m n", m=M2)
        STAGES = 3
        staging = [gram[:, 8 * i:8 * i + 8, :].rearrange("p a b -> p (a b)") for i in range(STAGES)]
        table_hi = sb("table_hi", [P, SELECTED, CHUNKS, D], fp32r)
        table_lo = sb("table_lo", [P, SELECTED, CHUNKS, D], fp32r)
        row_number_i = sb("row_number_i", [P, CHUNKS], i32)
        row_number = sb("row_number", [P, CHUNKS], fp32)
        ids_all = sb("ids_all", [P, SELECTED, PAIR], i32)
        one_hot = sb("one_hot", [P, RING, UNIT, PAIR], fp32r)
        dense_rows = sb("dense_rows", [P, HALVES, D], fp32)
        x_hi = sb("x_hi", [P, KC, GROUP], fp32r)
        x_lo = sb("x_lo", [P, KC, GROUP], fp32r)
        w1_hi = sb("w1_hi", [P, KC, HID1], fp32r)
        w1_lo = sb("w1_lo", [P, KC, HID1], fp32r)
        w2_hi = sb("w2_hi", [P, M1, HID2], fp32r)
        w2_lo = sb("w2_lo", [P, M1, HID2], fp32r)
        w3_sb = sb("w3_sb", [P, M2], fp32)
        b1_sb = sb("b1_sb", [P, M1], fp32)
        b2_sb = sb("b2_sb", [P, M2], fp32)
        h1_hi = sb("h1_hi", [P, M1, GROUP], fp32r)
        h1_lo = sb("h1_lo", [P, M1, GROUP], fp32r)
        y_sb = sb("y_sb", [1, GROUP], fp32)

        gram_ps = ctx.enter_context(nc.psum_tensor("gram_ps", [P, 2, BANK], fp32))
        stage_ps = ctx.enter_context(nc.psum_tensor("stage_ps", [P, 2 + FB, BANK], fp32))
        feat_ps = stage_ps[:, 2:2 + FB, :]

        ids_in = [sem(f"ids_in{h}") for h in range(HALVES)]
        dense_in = [sem(f"dense_in{s}") for s in range(2)]
        gathered = [[sem(f"gathered{s}_{k}") for k in range(TB)] for s in range(2)]
        gathers_begun = sem("gathers_begun")
        loads_begun = sem("loads_begun")
        dense_rows_in = sem("dense_rows_in")
        act_dma = sem("act_dma")
        weights_in = sem("weights_in")
        weights_hi = sem("weights_hi")
        weights_split = sem("weights_split")
        staged = [sem(f"staged{i}") for i in range(STAGES)]
        ids_all_in = sem("ids_all_in")
        row_number_written = sem("row_number_written")
        row_number_ready = sem("row_number_ready")
        one_hot_ready = sem("one_hot_ready")
        one_hot_used = sem("one_hot_used")
        identity_zero = sem("identity_zero")
        identity_ready = sem("identity_ready")
        gram_cleared = sem("gram_cleared")
        table_hi_ready = sem("table_hi_ready")
        table_split = sem("table_split")
        rows_transposed = sem("rows_transposed")
        feat_copied = [sem(f"feat_copied{b}") for b in range(FB)]
        gram_done = sem("gram_done")
        gram_copied = [sem(f"gram_copied{b}") for b in range(2)]
        stage_done = sem("stage_done")
        stage_copied = [sem(f"stage_copied{b}") for b in range(2 + FB)]
        x_hi_ready = sem("x_hi_ready")
        h1_hi_ready = sem("h1_hi_ready")
        h1_split = sem("h1_split")
        y_copied = sem("y_copied")

        block = ctx.enter_context(nc.Block())

        def wait(eng, semaphore, count):
            if not (isinstance(count, int) and count <= 0):
                eng.wait_ge(semaphore, count)

        def bank_features(k):
            return PER * k, min(RF, PER * (k + 1))

        def pair_steps(with_stages):
            t = [("table", x) for x in range(SELECTED)]
            n = ("next table", 0)
            r = [("rows", 0, k) for k in range(TB)]
            q = [("rows", 1, k) for k in range(TB)]
            g = [("gram", half, b) for half in range(2) for b in range(2)]
            s = [("stage", i) for i in range(SG)]
            if with_stages == "rest":
                return [t[0], r[0], t[1], s[13], r[1], t[2], r[2], t[3], s[14], r[3], t[4], r[4], t[5], s[15],
                        t[6], t[7], s[16], q[0], g[0], g[1],
                        q[1], q[2], q[3], s[17], q[4], n, g[2], g[3]]
            until_gram = [t[0], r[0], t[1], s[0], r[1], s[1], t[2], s[2], r[2], t[3], s[3], r[3], t[4], s[4],
                          r[4], s[5], t[5], s[6], t[6], s[7], t[7], s[8], q[0], s[9], g[0], s[10], g[1]]
            if with_stages == "all":
                return until_gram + [q[1], s[11], s[12], q[2], s[13], s[14],
                                     q[3], s[15], s[16], q[4], n, g[2], s[17], g[3]]
            if with_stages == "last":
                return until_gram + [q[1], s[11], q[2], q[3], s[12], q[4], s[13], g[2], g[3]]
            return until_gram + [q[1], s[11], q[2], q[3], s[12], q[4], n, g[2], g[3]]

        opened = [step for step in pair_steps("none")
                  if step[0] == "rows" or (step[0] == "table" and step[1] % 2 == 0)]
        assert len(opened) == PB

        def selected_bank(j, x):
            return PB * j + opened.index(("table", x - x % 2))

        def row_bank(j, half, k):
            return PB * j + opened.index(("rows", half, k))

        weights_after = [("table", 7), ("gram", 0, 1), ("rows", 1, 3), ("gram", 1, 1)]

        by_vector = [(0, TB - 1), (1, 1), (1, 3)]

        features_by_feature = features[:, :].rearrange("p (b f) -> p f b", f=F)

        LEFT = LAYER_1 + 3
        A, Z = BATCHES - 2, BATCHES - 1
        after_pairs = [(A, LEFT), (Z, 0), (Z, 1), (Z, 2), (Z, 3), (Z, 4), (Z, 5), (Z, 6), (Z, DENSE),
                       (A, LAYER_2), (A, LAYER_2 + 1), (Z, TO_COLUMNS), (Z, TO_COLUMNS + 1), (Z, TO_COLUMNS + 2),
                       (A, LAYER_3)] + [(Z, i) for i in range(LAYER_1, SG)]
        last_stages = [(A, i) for i in range(LEFT)] + after_pairs
        assert sorted(last_stages) == [(B, i) for B in (A, Z) for i in range(SG)]
        last_banks = [i % 2 for i in range(LEFT)] + [(2 + n) % (2 + FB) for n in range(len(after_pairs))]

        def of_last(B):
            return isinstance(B, int) and B >= A

        def stage_count(B, i):
            return SG * A + last_stages.index((B, i)) + 1 if of_last(B) else SG * B + i + 1

        def stage_bank(B, i):
            return last_banks[last_stages.index((B, i))] if of_last(B) else i % 2

        def stage_turn(B, i):
            if not of_last(B):
                return SG // 2 * B + i // 2 + 1
            at = last_stages.index((B, i))
            return (SG // 2 * A if last_banks[at] < 2 else 0) + last_banks[0:at + 1].count(last_banks[at])

        def pairs_of(B):
            if of_last(B) and B == Z:
                return features[:, 0:QUADS * PAIRS].rearrange("p (s z) -> p s z", s=QUADS)
            return pairs

        def batch_columns(B):
            if isinstance(B, int) and B == 0:
                return 0, P // 2
            if isinstance(B, int) and B == BATCHES - 1:
                return P // 2, P // 2
            return 0, P

        w1_pairs = w1[0:PAIRS, :].rearrange("(c k) n -> k c n", k=ZK)

        def scratch_as(parts, c, n):
            return scratch[0:parts, 0:c * n].rearrange("p (c n) -> p c n", c=c)

        weights = [(w1_pairs[:, 0:2, :], scratch_as(ZK, 2, HID1), w1_hi[0:ZK, 0:2, :], w1_lo[0:ZK, 0:2, :]),
                   (w1_pairs[:, 2:3, :], scratch_as(ZK, 1, HID1), w1_hi[0:ZK, 2:3, :], w1_lo[0:ZK, 2:3, :]),
                   (w1[PAIRS:PAIRS + D, :], scratch[:, 0:HID1], w1_hi[:, ZC, :], w1_lo[:, ZC, :]),
                   (w2.rearrange("(c k) n -> k c n", k=P), scratch_as(P, M1, HID2), w2_hi[:, :, :], w2_lo[:, :, :])]

        @block.sync
        def _(sp):
            def wait_apart(semaphore, count):
                wait(sp, semaphore, count)
                sp.sem_inc(loads_begun, 1)

            def load_half(G, h):
                r0 = G * GROUP + h * P
                wait_apart(rows_transposed, TB * (HALVES * G + h - 3))
                sp.dma_start(ids_sb[:, h, :], ids[bass.ds(r0, P), :]).then_inc(ids_in[h], 16)
                wait_apart(rows_transposed, TB * (HALVES * G + h - 2) + 1)
                sp.dma_start(rows[:, h % 2, 0, :], dense[bass.ds(r0, P), :]).then_inc(dense_in[h % 2], 16)

            def load_ids_all(G, j):
                r0 = G * GROUP + j * PAIR
                wait_apart(one_hot_ready, UNITS * (2 * G + j))
                sp.dma_start(ids_all[:, :, :],
                             ids_by_table[:, bass.ds(r0, PAIR)].partition_broadcast(P)
                             ).then_inc(ids_all_in, 16)

            def load_dense_rows(G, j):
                r0 = G * GROUP + j * PAIR
                wait_apart(stage_done, stage_count(G - 1 + j, DENSE) if not isinstance(G, int) or G > 0 else 0)
                sp.dma_start(dense_rows[:, 2 * j:2 * j + 2, :],
                             dense[bass.ds(r0, PAIR), :].rearrange("(h p) d -> p h d", p=P)
                             ).then_inc(dense_rows_in, 16)

            def load_weights(n):
                wait(sp, weights_split, n)
                sp.dma_start(weights[n][1], weights[n][0]).then_inc(weights_in, 16)

            load_half(0, 0)
            for x in range(SELECTED):
                wait(sp, table_split, x - STAGES + 1)
                table = select_tables[x].rearrange("(p c) d -> p (c d)", c=CHUNKS)
                for p0, p1 in ((0, TP // 16 * 16), (TP // 16 * 16, TP)):
                    sp.dma_start(staging[x % STAGES][p0:p1, :], table[p0:p1, :]).then_inc(staged[x % STAGES], 16)
                if x == 0:
                    load_ids_all(0, 0)
                if x == 1:
                    load_half(0, 1)
                if x == 4:
                    load_half(0, 2)
                if x == 6:
                    load_weights(0)
            load_ids_all(0, 1)
            load_weights(1)
            load_half(0, 3)
            load_weights(2)
            load_dense_rows(0, 0)
            load_weights(3)
            with sp.Fori(1, GROUPS) as G:
                load_half(G, 0)
                load_ids_all(G, 0)
                load_half(G, 1)
                load_dense_rows(G, 0)
                load_half(G, 2)
                load_ids_all(G, 1)
                load_dense_rows(G - 1, 1)
                load_half(G, 3)
            load_dense_rows(GROUPS - 1, 1)

        @block.gpsimd
        def _(pool):
            nc.gpsimd.memset(identity[:, :], 0.0).then_inc(identity_zero, 1)
            pool.wait_ge(identity_zero, 1)
            nc.gpsimd.affine_select(out=identity[:, :], in_=identity[:, :], compare_op=ALU.not_equal, fill=1.0,
                                    base=0, pattern=[[-1, P]], channel_multiplier=1).then_inc(identity_ready, 1)

            nc.gpsimd.iota(row_number_i[:, :], pattern=[[1, CHUNKS]], base=0, channel_multiplier=CHUNKS
                           ).then_inc(row_number_written, 1)

            def gathers(G):
                for h in range(HALVES):
                    pool.wait_ge(ids_in[h], 16 * G + 16)
                    for k in range(TB):
                        wait(pool, rows_transposed, TB * (HALVES * G + h - 2) + k + 1)
                        nc.gpsimd.sem_inc(gathers_begun, 1)
                        first, end = bank_features(k)
                        for f in range(max(first, 1), end):
                            nc.gpsimd.indirect_dma_start(
                                rows[:, h % 2, f, :], None, gather_tables[f - 1],
                                bass.IndirectOffsetOnAxis(ids_sb[:, h, f - 1:f], 0)
                            ).then_inc(gathered[h % 2][k], 16)

            gathers(0)
            with pool.Fori(1, GROUPS) as G:
                gathers(G)

        @block.tensor
        def _(pe):
            def transpose_rows(G, j, half, k):
                use = 2 * G + j + 1
                i = row_bank(j, half, k)
                first, end = bank_features(k)
                if k == 0:
                    pe.wait_ge(dense_in[half], 16 * use)
                pe.wait_ge(gathered[half][k], 16 * (end - max(first, 1)) * use)
                wait(pe, feat_copied[i % FB], TG // FB * G + i // FB)
                for f in range(first, end):
                    last = nc.tensor.transpose(feat_ps[:, i % FB, (f - first) * P:(f - first + 1) * P],
                                               rows[:, half, f, :], identity[:, :])
                last.then_inc(rows_transposed, 1)

            def select_feature(G, j, x):
                i = selected_bank(j, x)
                if x % 2 == 0:
                    wait(pe, feat_copied[i % FB], TG // FB * G + i // FB)
                if isinstance(G, int) and G == 0 and j == 0:
                    pe.wait_ge(table_split, x + 1)
                for c in range(CHUNKS):
                    u = UNITS * j + (x * CHUNKS + c) // UNIT
                    if c % UNIT == 0:
                        pe.wait_ge(one_hot_ready, 2 * UNITS * G + u + 1)
                    for table in (table_hi, table_lo):
                        last = nc.tensor.matmul(feat_ps[:, i % FB, (x % 2) * PAIR:(x % 2 + 1) * PAIR],
                                                table[0:TP, x, c, :], one_hot[0:TP, u % RING, c % UNIT, :],
                                                start=(c == 0 and table is table_hi),
                                                stop=(c == CHUNKS - 1 and table is table_lo))
                    if c % UNIT == UNIT - 1:
                        last.then_inc(one_hot_used, 1)

            def gram_matrices(G, j, half, b):
                h = 2 * j + half
                if b == 0:
                    needed = [row_bank(j, half, TB - 1)] + [selected_bank(j, x) for x in range(SELECTED)]
                    for r in range(FB):
                        pe.wait_ge(feat_copied[r], TG // FB * G + (max(needed) - r + FB) // FB)
                wait(pe, gram_copied[b], HALVES * G + h)
                for m in range(NB):
                    for s in range(QUADS):
                        at = (P * half + QUADS * (NB * b + m) + s) * F
                        last = nc.tensor.matmul(gram_ps[Q * s:Q * s + FC, b, m * FC:(m + 1) * FC],
                                                features[:, at:at + FC], features[:, at + 1:at + F],
                                                start=True, stop=True)
                last.then_inc(gram_done, 1)

            def stage_bank_free(B, i):
                wait(pe, stage_copied[stage_bank(B, i)], stage_turn(B, i) - 1)

            def pairs_to_rows(B, k):
                n0, N = batch_columns(B)
                if k == 0:
                    for b in range(2):
                        pe.wait_ge(gram_copied[b], HALVES * B + (2 if n0 == 0 else 0))
                stage_bank_free(B, k)
                for n, g in enumerate(range(1 + PER * k, min(F, 1 + PER * (k + 1)))):
                    last = nc.tensor.transpose(stage_ps[0:N, stage_bank(B, k), n * P:(n + 1) * P], gram[:, g - 1, n0:n0 + N],
                                               identity[:, :])
                last.then_inc(stage_done, 1)

            def pairs_to_columns(B, c):
                n0, N = batch_columns(B)
                if c == 0:
                    for k in range(0 if of_last(B) else ZB - 2, ZB):
                        pe.wait_ge(stage_copied[stage_bank(B, k)], stage_turn(B, k))
                i = TO_COLUMNS + c
                stage_bank_free(B, i)
                for s in range(QUADS):
                    last = nc.tensor.transpose(stage_ps[0:ZK, stage_bank(B, i), s * N:(s + 1) * N],
                                               pairs_of(B)[0:N, s, c * ZK:(c + 1) * ZK], identity[0:N, 0:N])
                last.then_inc(stage_done, 1)

            def dense_to_columns(B):
                n0, N = batch_columns(B)
                pe.wait_ge(dense_rows_in, 16 * (2 * B + (1 if n0 == 0 else 0)))
                stage_bank_free(B, DENSE)
                for h in range(N // Q):
                    last = nc.tensor.transpose(stage_ps[:, stage_bank(B, DENSE), h * P:(h + 1) * P],
                                               dense_rows[:, n0 // Q + h, :], identity[:, :])
                last.then_inc(stage_done, 1)

            def split_products(out, w_hi, w_lo, x_hi, x_lo, chunks, width, rows_of, wait_for_chunk):
                steps = [(c, w, x) for c in chunks for w, x in ((w_hi, x_hi), (w_hi, x_lo), (w_lo, x_hi))]
                for n, (c, w, x) in enumerate(steps):
                    k = rows_of(c)
                    if n % 3 == 0:
                        wait_for_chunk(c)
                    last = nc.tensor.matmul(out, w(c, k), x[0:k, c, 0:width], start=(n == 0), stop=(n == len(steps) - 1))
                return last

            def layer_1(B, m):
                W = QUADS * batch_columns(B)[1]

                def wait_for_chunk(c):
                    if m == 0:
                        i = TO_COLUMNS + c if c < ZC else DENSE
                        pe.wait_ge(stage_copied[stage_bank(B, i)], stage_turn(B, i))

                if isinstance(B, int) and B == 0 and m == 0:
                    pe.wait_ge(weights_split, len(weights))
                    pe.wait_ge(act_dma, 3 * 16)
                stage_bank_free(B, LAYER_1 + m)
                cols = slice(m * P, (m + 1) * P)
                split_products(stage_ps[:, stage_bank(B, LAYER_1 + m), 0:W], lambda c, k: w1_hi[0:k, c, cols],
                               lambda c, k: w1_lo[0:k, c, cols], x_hi, x_lo, [ZC, *range(ZC)], W,
                               lambda c: ZK if c < ZC else D, wait_for_chunk).then_inc(stage_done, 1)

            def layer_2(B, m):
                W = QUADS * batch_columns(B)[1]

                def wait_for_chunk(c):
                    if m == 0:
                        pe.wait_ge(h1_split, M1 * B + c + 1)

                stage_bank_free(B, LAYER_2 + m)
                cols = slice(m * P, (m + 1) * P)
                split_products(stage_ps[:, stage_bank(B, LAYER_2 + m), 0:W], lambda c, k: w2_hi[0:k, c, cols],
                               lambda c, k: w2_lo[0:k, c, cols], h1_hi, h1_lo, range(M1), W,
                               lambda c: P, wait_for_chunk).then_inc(stage_done, 1)

            def layer_3(B):
                W = QUADS * batch_columns(B)[1]
                stage_bank_free(B, LAYER_3)
                for m in range(M2):
                    i = LAYER_2 + m
                    pe.wait_ge(stage_copied[stage_bank(B, i)], stage_turn(B, i))
                    last = nc.tensor.matmul(stage_ps[0:1, stage_bank(B, LAYER_3), 0:W], w3_sb[:, m:m + 1], h2[:, m, 0:W],
                                            start=(m == 0), stop=(m == M2 - 1))
                last.then_inc(stage_done, 1)

            def stage(B, i):
                if i < DENSE:
                    pairs_to_rows(B, i)
                elif i == DENSE:
                    dense_to_columns(B)
                elif i < LAYER_1:
                    pairs_to_columns(B, i - TO_COLUMNS)
                elif i < LAYER_2:
                    layer_1(B, i - LAYER_1)
                elif i < LAYER_3:
                    layer_2(B, i - LAYER_2)
                else:
                    layer_3(B)

            def pair(G, j, with_stages, B):
                for kind, *at in pair_steps(with_stages):
                    if kind == "table":
                        if at[0] > 0:
                            select_feature(G, j, *at)
                    elif kind == "next table":
                        select_feature(G, j + 1, *at)
                    elif kind == "rows":
                        transpose_rows(G, j, *at)
                    elif kind == "gram":
                        gram_matrices(G, j, *at)
                    elif with_stages != "none":
                        stage(B, *at)

            pe.wait_ge(identity_ready, 1)
            pe.wait_ge(gram_cleared, 1)
            select_feature(0, 0, 0)
            pair(0, 0, "none", None)
            pair(0, 1, "all", 0)
            pair(1, 0, "none", None)
            with pe.Fori(1, GROUPS - 1) as B:
                pair(B, 1, "first", B)
                pair(B + 1, 0, "rest", B)
            pair(GROUPS - 1, 1, "last", GROUPS - 1)
            for B, i in after_pairs:
                stage(B, i)

        def copy_rows(eng, copy, G, j, half, k):
            i = row_bank(j, half, k)
            h = 2 * j + half
            first, end = bank_features(k)
            eng.wait_ge(rows_transposed, TB * (HALVES * G + h) + k + 1)
            wait(eng, gram_done, 2 * (HALVES * G + h - 1))
            copy(features_by_feature[:, first:end, half * P:(half + 1) * P],
                 feat_ps[:, i % FB, 0:(end - first) * P].rearrange("p (f b) -> p f b", b=P)
                 ).then_inc(feat_copied[i % FB], 1)

        def copy_gram(eng, copy, b, G, j, half):
            h = 2 * j + half
            eng.wait_ge(gram_done, 2 * HALVES * G + 2 * h + b + 1)
            wait(eng, stage_done, stage_count(G - 1 + j, ZB - 1) if not isinstance(G, int) or G > 0 else 0)
            n0 = h * Q + b * NB
            copy(gram[:, :, n0:n0 + NB], gram_ps[:, b, 0:NB * FC].rearrange("p (n g) -> p g n", g=FC)
                 ).then_inc(gram_copied[b], 1)

        def copy_pair_rows(eng, copy, B, k):
            N = batch_columns(B)[1]
            eng.wait_ge(stage_done, stage_count(B, k))
            for n, g in enumerate(range(1 + PER * k, min(F, 1 + PER * (k + 1)))):
                last = copy(pairs_of(B)[0:N, :, pair_at[g]:pair_at[g] + g],
                            stage_ps[0:N, stage_bank(B, k), n * P:(n + 1) * P].rearrange("p (s f) -> p s f", f=Q)[:, :, 0:g])
            last.then_inc(stage_copied[stage_bank(B, k)], 1)

        @block.scalar
        def _(act):
            def copy(dst, src):
                return nc.scalar.copy(dst, src)

            def high_x(B, c):
                W = QUADS * batch_columns(B)[1]
                i = TO_COLUMNS + c if c < ZC else DENSE
                act.wait_ge(stage_done, stage_count(B, i))
                if c < ZC:
                    nc.scalar.copy(x_hi[0:ZK, c, 0:W], stage_ps[0:ZK, stage_bank(B, TO_COLUMNS + c), 0:W]
                                   ).then_inc(x_hi_ready, 1)
                else:
                    nc.scalar.copy(x_hi[:, ZC, 0:W].rearrange("p (s n) -> p s n", s=QUADS),
                                   stage_ps[:, stage_bank(B, DENSE), 0:W].rearrange("p (n s) -> p s n", s=QUADS)
                                   ).then_inc(x_hi_ready, 1)

            def relu_1(B, m):
                W = QUADS * batch_columns(B)[1]
                i = LAYER_1 + m
                act.wait_ge(stage_done, stage_count(B, i))
                if m >= 2:
                    act.wait_ge(h1_split, M1 * B + m - 1)
                nc.scalar.activation(relu1[:, m % 2, 0:W], stage_ps[:, stage_bank(B, i), 0:W], ACT.Relu,
                                     bias=b1_sb[:, m:m + 1]).then_inc(stage_copied[stage_bank(B, i)], 1)

            def relu_2(B, m):
                W = QUADS * batch_columns(B)[1]
                i = LAYER_2 + m
                act.wait_ge(stage_done, stage_count(B, i))
                nc.scalar.activation(h2[:, m, 0:W], stage_ps[:, stage_bank(B, i), 0:W], ACT.Relu,
                                     bias=b2_sb[:, m:m + 1]).then_inc(stage_copied[stage_bank(B, i)], 1)

            def store_y(B):
                n0, N = batch_columns(B)
                W = QUADS * N
                act.wait_ge(stage_done, stage_count(B, LAYER_3))
                act.wait_ge(act_dma, 16 * (2 * B - 1) + 3 * 16 if not isinstance(B, int) or B > 0 else 3 * 16)
                nc.scalar.copy(y_sb[0:1, 0:W].rearrange("p (n s) -> p s n", s=QUADS),
                               stage_ps[0:1, stage_bank(B, LAYER_3), 0:W].rearrange("p (s n) -> p s n", s=QUADS)
                               ).then_inc(stage_copied[stage_bank(B, LAYER_3)], 1)
                act.wait_ge(stage_copied[stage_bank(B, LAYER_3)], stage_turn(B, LAYER_3))
                for n in range(n0, n0 + N, P // 2):
                    r0 = B * GROUP if n == 0 else B * GROUP - PAIR
                    act.dma_start(out[bass.ds(r0, PAIR), :].rearrange("(o n) i -> o (n i)", o=1),
                                  y_sb[:, QUADS * (n - n0):QUADS * (n - n0) + PAIR]).then_inc(act_dma, 16)

            def copy_selected(G, j, x):
                i = selected_bank(j, x)
                n = x % 2 + 1
                act.wait_ge(one_hot_used, 2 * UNITS * G + UNITS * j + (x + 1) * CHUNKS // UNIT)
                wait(act, gram_done, 2 * (HALVES * G + 2 * j))
                nc.scalar.copy(features_by_feature[:, RF + x + 1 - n:RF + x + 1, :],
                               feat_ps[:, i % FB, 0:n * PAIR].rearrange("p (f b) -> p f b", b=PAIR)
                               ).then_inc(feat_copied[i % FB], 1)

            def high_table(x):
                act.wait_ge(staged[x % STAGES], 2 * 16 * (x // STAGES + 1))
                nc.scalar.copy(table_hi[0:TP, x, :, :].rearrange("p c d -> p (c d)"), staging[x % STAGES][0:TP, :]
                               ).then_inc(table_hi_ready, 1)

            def high_weights(n):
                act.wait_ge(weights_in, 16 * n + 16)
                nc.scalar.copy(weights[n][2], weights[n][1]).then_inc(weights_hi, 1)

            def stage(B, i):
                if i < DENSE:
                    if i % 2 == 0:
                        if isinstance(B, int) and B == 0 and i == 0:
                            act.wait_ge(weights_split, len(weights))
                        copy_pair_rows(act, copy, B, i)
                elif i < LAYER_1:
                    high_x(B, i - TO_COLUMNS if i > DENSE else ZC)
                elif i < LAYER_2:
                    relu_1(B, i - LAYER_1)
                elif i < LAYER_3:
                    relu_2(B, i - LAYER_2)
                else:
                    store_y(B)

            def pair(G, j, with_stages, B, first=False):
                for kind, *at in pair_steps(with_stages):
                    if kind == "table":
                        x, = at
                        if x % 2 == 1 or x == SELECTED - 1:
                            copy_selected(G, j, x)
                        if first and x + 2 < SELECTED:
                            high_table(x + 2)
                    elif kind == "rows":
                        if tuple(at) not in by_vector:
                            copy_rows(act, copy, G, j, *at)
                    elif kind == "gram":
                        half, b = at
                        if b == 0:
                            if first and half == 0:
                                act.wait_ge(table_split, SELECTED)
                            copy_gram(act, copy, 0, G, j, half)
                    elif kind == "stage" and with_stages != "none":
                        stage(B, *at)
                    if first and (kind, *at) in weights_after:
                        high_weights(weights_after.index((kind, *at)))

            high_table(0)
            high_table(1)
            act.dma_start(b1_sb[:, :], b1.rearrange("(m p) -> p m", p=P), allow_slow_non_contiguous=True).then_inc(act_dma, 16)
            act.dma_start(b2_sb[:, :], b2.rearrange("(m p) -> p m", p=P), allow_slow_non_contiguous=True).then_inc(act_dma, 16)
            act.dma_start(w3_sb[:, :], w3.rearrange("(m p) o -> p (m o)", p=P), allow_slow_non_contiguous=True).then_inc(act_dma, 16)
            pair(0, 0, "none", None, first=True)
            pair(0, 1, "all", 0)
            pair(1, 0, "none", None)
            with act.Fori(1, GROUPS - 1) as B:
                pair(B, 1, "first", B)
                pair(B + 1, 0, "rest", B)
            pair(GROUPS - 1, 1, "last", GROUPS - 1)
            for B, i in after_pairs:
                stage(B, i)
            act.wait_ge(act_dma, 16 * 2 * GROUPS + 3 * 16)

        @block.vector
        def _(dve):
            def copy(dst, src):
                return nc.vector.tensor_copy(dst, src)

            def low_part(lo, whole, hi):
                return nc.vector.tensor_tensor(lo, whole, hi.bitcast(fp32), ALU.subtract)

            def low_x(B, c):
                W = QUADS * batch_columns(B)[1]
                dve.wait_ge(x_hi_ready, KC * B + (c + 1) % KC + 1)
                if c < ZC:
                    low_part(x_lo[0:ZK, c, 0:W], stage_ps[0:ZK, stage_bank(B, TO_COLUMNS + c), 0:W], x_hi[0:ZK, c, 0:W]
                             ).then_inc(stage_copied[stage_bank(B, TO_COLUMNS + c)], 1)
                else:
                    low_part(x_lo[:, ZC, 0:W].rearrange("p (s n) -> p s n", s=QUADS),
                             stage_ps[:, stage_bank(B, DENSE), 0:W].rearrange("p (n s) -> p s n", s=QUADS),
                             x_hi[:, ZC, 0:W].rearrange("p (s n) -> p s n", s=QUADS)
                             ).then_inc(stage_copied[stage_bank(B, DENSE)], 1)

            def split_h1(B, m):
                W = QUADS * batch_columns(B)[1]
                i = LAYER_1 + m
                dve.wait_ge(stage_copied[stage_bank(B, i)], stage_turn(B, i))
                nc.vector.tensor_copy(h1_hi[:, m, 0:W], relu1[:, m % 2, 0:W]).then_inc(h1_hi_ready, 1)
                dve.wait_ge(h1_hi_ready, M1 * B + m + 1)
                low_part(h1_lo[:, m, 0:W], relu1[:, m % 2, 0:W], h1_hi[:, m, 0:W]).then_inc(h1_split, 1)

            def write_one_hot(G, j, x):
                for v in range(x * CHUNKS // UNIT, (x + 1) * CHUNKS // UNIT):
                    u = UNITS * j + v
                    if v == 0:
                        dve.wait_ge(ids_all_in, 16 * (2 * G + j + 1))
                    wait(dve, one_hot_used, 2 * UNITS * G + u - RING + 1)
                    for c in range(UNIT):
                        chunk = (v * UNIT + c) % CHUNKS
                        last = nc.vector.tensor_scalar(one_hot[0:TP, u % RING, c, :], ids_all[0:TP, x, :],
                                                       row_number[0:TP, chunk:chunk + 1], None, ALU.is_equal)
                    last.then_inc(one_hot_ready, 1)

            def low_table(x):
                dve.wait_ge(table_hi_ready, x + 1)
                low_part(table_lo[0:TP, x, :, :].rearrange("p c d -> p (c d)"), staging[x % STAGES][0:TP, :],
                         table_hi[0:TP, x, :, :].rearrange("p c d -> p (c d)")).then_inc(table_split, 1)

            def low_weights(n):
                dve.wait_ge(weights_hi, n + 1)
                low_part(weights[n][3], weights[n][1], weights[n][2]).then_inc(weights_split, 1)

            def stage(B, i):
                if i < DENSE:
                    if i % 2 == 1:
                        if isinstance(B, int) and B == 0 and i == 1:
                            dve.wait_ge(weights_split, len(weights))
                        copy_pair_rows(dve, copy, B, i)
                elif i < LAYER_1:
                    low_x(B, i - TO_COLUMNS if i > DENSE else ZC)
                elif i < LAYER_2:
                    split_h1(B, i - LAYER_1)

            def vector_steps(with_stages):
                t = [("table", x) for x in range(SELECTED)]
                n = [("next table", x) for x in range(2)]
                r = [("rows", 0, k) for k in range(TB)]
                q = [("rows", 1, k) for k in range(TB)]
                g = [("gram", half, b) for half in range(2) for b in range(2)]
                s = [("stage", i) for i in range(SG)]
                if with_stages == "rest":
                    return [t[2], t[3], s[13], t[4], t[5], s[14], t[6], r[4], t[7], n[0], g[1],
                            q[1], q[3], n[1], g[3]]
                until_gram = [t[2], s[1], t[3], t[4], s[3], t[5], r[4], s[5], t[6], t[7], s[7], s[8], s[9], n[0],
                              s[10], g[1]]
                if with_stages == "all":
                    return until_gram + [q[1], s[11], s[12], s[13], s[14],
                                         q[3], n[1], g[3]]
                if with_stages == "last":
                    return until_gram[:-3] + [s[10], g[1], q[1], s[11], q[3], s[12], s[13], g[3]]
                return until_gram + [q[1], s[11], q[3], s[12], n[1], g[3]]

            def pair(G, j, with_stages, B, first=False):
                for kind, *at in vector_steps(with_stages):
                    if kind == "table":
                        if first:
                            low_table(*at)
                        write_one_hot(G, j, *at)
                    elif kind == "next table":
                        write_one_hot(G, j + 1, *at)
                    elif kind == "rows":
                        assert tuple(at) in by_vector
                        copy_rows(dve, copy, G, j, *at)
                    elif kind == "gram":
                        half, b = at
                        copy_gram(dve, copy, b, G, j, half)
                    elif with_stages != "none":
                        stage(B, *at)
                    if first and (kind, *at) in weights_after:
                        low_weights(weights_after.index((kind, *at)))

            nc.vector.memset(gram_ps[:, :, :], 0.0).then_inc(gram_cleared, 1)
            dve.wait_ge(row_number_written, 1)
            nc.vector.tensor_copy(row_number[:, :], row_number_i[:, :]).then_inc(row_number_ready, 1)
            dve.wait_ge(row_number_ready, 1)
            for x in range(2):
                low_table(x)
                write_one_hot(0, 0, x)
            pair(0, 0, "none", None, first=True)
            pair(0, 1, "all", 0)
            pair(1, 0, "none", None)
            with dve.Fori(1, GROUPS - 1) as B:
                pair(B, 1, "first", B)
                pair(B + 1, 0, "rest", B)
            pair(GROUPS - 1, 1, "last", GROUPS - 1)
            for B, i in after_pairs:
                stage(B, i)


SELECT_TABLES, SELECT_ROWS = 8, 1000


def kernel(**inputs):
    import numpy as _np
    import concourse.bacc as _bacc
    from concourse import mybir as _mybir
    from concourse.bass_utils import run_bass_kernel_spmd as _run

    nc = _bacc.Bacc("TRN2", target_bir_lowering=False, num_devices=1)
    n_tables = sum(name.startswith("tbl_") for name in inputs)
    small = [t for t in range(n_tables) if inputs[f"tbl_{t}"].shape[0] == SELECT_ROWS]
    selected = small[:SELECT_TABLES]
    gathered = [t for t in range(n_tables) if t not in selected]
    feature = [0] + [t + 1 for t in gathered + selected]
    n = len(feature)
    order = []
    for g in range(n):
        for f in range(g):
            a, b = sorted((feature[f], feature[g]))
            order.append(a * n - a * (a + 1) // 2 + b - a - 1)
    w1 = _np.ascontiguousarray(inputs["W_top1"])
    order = _np.array(order + list(range(len(order), w1.shape[0])))
    arrays = {}

    def give(name, a):
        a = _np.ascontiguousarray(a)
        arrays[f"in_{name}"] = a
        return nc.dram_tensor(f"in_{name}", a.shape, _mybir.dt.from_np(a.dtype), kind="ExternalInput").ap()

    all_ids = _np.ascontiguousarray(inputs["ids"])
    dense = give("dense", inputs["r_dense_features"])
    ids = give("ids", all_ids[:, gathered])
    ids_by_table = give("ids_by_table", all_ids[:, selected].T)
    gather_tables = [give(f"tbl_{t}", inputs[f"tbl_{t}"]) for t in gathered]
    select_tables = [give(f"tbl_{t}", inputs[f"tbl_{t}"]) for t in selected]
    w1 = give("w1", w1[order])
    b1, w2, b2, w3 = (give(n, inputs[n]) for n in ("b_top1", "W_top2", "b_top2", "W_top3"))
    out = nc.dram_tensor("out_y", (all_ids.shape[0], 1), _mybir.dt.float32, kind="ExternalOutput").ap()
    dlrm_tower_kernel(nc, dense, ids, gather_tables, ids_by_table, select_tables, w1, b1, w2, b2, w3, out)
    r = _run(nc, [arrays], core_ids=[0])
    return r.results[0]["out_y"]
```
